# Optimizing a Trainium2 kernel written in Bass

```python
import numpy as np
import jax
import jax.numpy as jnp

def _softmax(x, axis=-1):
    return jax.nn.softmax(x, axis=axis)

def _gelu(x):
    return jax.nn.gelu(x, approximate=True)

def _silu(x):
    return jax.nn.silu(x)

def _sigmoid(x):
    return jax.nn.sigmoid(x)

def _layernorm(x, axis=-1, eps=1e-05):
    m = jnp.mean(x, axis=axis, keepdims=True)
    v = jnp.var(x, axis=axis, keepdims=True)
    return (x - m) / jnp.sqrt(v + eps)

def _scatter_add(tgt, idx, src, axis=0):
    return tgt.at[idx].add(src)

def _segment_sum(src, seg, n):
    return jax.ops.segment_sum(src, seg, n)
kernel_name = 'mk_gnn_ffn_d1_gnn_r8_dda430'

def setup_inputs(seed: int=0):
    np.random.seed(seed)
    _w = jnp.asarray

    def _rec_inputs():
        import jax
        import jax.numpy as jnp
        _gk = jax.random.key(seed)
        x = -0.0002928 + 1 * jax.random.normal(jax.random.fold_in(_gk, 1), (6250, 256), jnp.float32)
        src = jax.random.randint(jax.random.fold_in(_gk, 2), (200000,), 0, 6250, jnp.int32)
        dst = jax.random.randint(jax.random.fold_in(_gk, 3), (200000,), 0, 6250, jnp.int32)
        _o = jnp.argsort(dst, stable=True)
        src = src[_o]
        dst = dst[_o]
        return (x, src, dst)
    x, src, dst = _rec_inputs()

    def _L0_gnn_setup():
        import jax, jax.numpy as jnp
        import numpy as np
        V = 2048
        G = 32
        D = 256
        N = 8
        H = 32
        I = 1024
        LN_EPS = 1e-12

        def _layer_norm(x, g, b):
            mu = jnp.mean(x, axis=-1, keepdims=True)
            var = jnp.mean(jnp.square(x - mu), axis=-1, keepdims=True)
            return (x - mu) * jax.lax.rsqrt(var + LN_EPS) * g + b
        key = jax.random.key(seed)
        ks = jax.random.split(key, 5)
        node_embeddings = jax.random.normal(ks[0], (V, D), jnp.float32)
        idx = np.arange(V, dtype=np.int32).reshape(-1, G)
        src = np.repeat(idx, G, axis=1).reshape(-1)
        dst = np.tile(idx, (1, G)).reshape(-1)
        in_graph_node_pairs = jnp.asarray(np.stack([src, dst], axis=-1))
        s = 0.02
        return {'node_embeddings': node_embeddings, 'in_graph_node_pairs': in_graph_node_pairs, 'W_qkv': jax.random.normal(ks[1], (D, 3 * N * H), jnp.float32) * s, 'W_o': jax.random.normal(ks[2], (N * H, D), jnp.float32) * s, 'ln1_g': jnp.ones((D,), jnp.float32), 'ln1_b': jnp.zeros((D,), jnp.float32), 'W_i': jax.random.normal(ks[3], (D, I), jnp.float32) * s, 'W_out2': jax.random.normal(ks[4], (I, D), jnp.float32) * s, 'ln2_g': jnp.ones((D,), jnp.float32), 'ln2_b': jnp.zeros((D,), jnp.float32)}
    _L0_gnn_all = _L0_gnn_setup()
    _L0_gnn_in = {k: v for k, v in _L0_gnn_all.items() if k in ('W_qkv', 'W_o', 'ln1_g', 'ln1_b', 'W_i', 'W_out2', 'ln2_g', 'ln2_b')}
    del _L0_gnn_all

    def _L0_ffn_setup():
        import jax, jax.numpy as jnp
        import numpy as np
        B, A = (512, 8)
        IN, OUT = (256, 256)
        SH1, SH2 = (256, 128)
        EH1, EH2 = (128, 64)
        E, TOPK = (4, 2)

        def _shared_mlp(x, W1, b1, W2, b2, W3, b3):
            h = jax.nn.relu(x @ W1 + b1)
            h = jax.nn.relu(h @ W2 + b2)
            return h @ W3 + b3

        def _experts_mlp(x, eW1, eb1, eW2, eb2, eW3, eb3):
            h = jax.nn.relu(jnp.einsum('baf,efh->ebah', x, eW1) + eb1[:, None, None, :])
            h = jax.nn.relu(jnp.einsum('ebah,ehg->ebag', h, eW2) + eb2[:, None, None, :])
            o = jnp.einsum('ebag,ego->ebao', h, eW3) + eb3[:, None, None, :]
            return jnp.moveaxis(o, 0, -1)
        key = jax.random.key(seed)
        ks = jax.random.split(key, 16)
        s = 0.05
        return {'x': jax.random.normal(ks[0], (B, A, IN), jnp.float32), 'sW1': jax.random.normal(ks[1], (IN, SH1), jnp.float32) * s, 'sb1': jnp.zeros((SH1,), jnp.float32), 'sW2': jax.random.normal(ks[2], (SH1, SH2), jnp.float32) * s, 'sb2': jnp.zeros((SH2,), jnp.float32), 'sW3': jax.random.normal(ks[3], (SH2, OUT), jnp.float32) * s, 'sb3': jnp.zeros((OUT,), jnp.float32), 'eW1': jax.random.normal(ks[4], (E, IN, EH1), jnp.float32) * s, 'eb1': jnp.zeros((E, EH1), jnp.float32), 'eW2': jax.random.normal(ks[5], (E, EH1, EH2), jnp.float32) * s, 'eb2': jnp.zeros((E, EH2), jnp.float32), 'eW3': jax.random.normal(ks[6], (E, EH2, OUT), jnp.float32) * s, 'eb3': jnp.zeros((E, OUT), jnp.float32), 'gW': jax.random.normal(ks[7], (IN, E), jnp.float32) * s, 'gb': jnp.zeros((E,), jnp.float32)}
    _L0_ffn_all = _L0_ffn_setup()
    _L0_ffn_in = {k: v for k, v in _L0_ffn_all.items() if k in ('sW1', 'sb1', 'sW2', 'sb2', 'sW3', 'sb3', 'eW1', 'eb1', 'eW2', 'eb2', 'eW3', 'eb3', 'gW', 'gb')}
    del _L0_ffn_all
    return {'x': x, 'src': src, 'dst': dst, 'L0_gnn_W_qkv': _L0_gnn_in['W_qkv'], 'L0_gnn_W_o': _L0_gnn_in['W_o'], 'L0_gnn_ln1_g': _L0_gnn_in['ln1_g'], 'L0_gnn_ln1_b': _L0_gnn_in['ln1_b'], 'L0_gnn_W_i': _L0_gnn_in['W_i'], 'L0_gnn_W_out2': _L0_gnn_in['W_out2'], 'L0_gnn_ln2_g': _L0_gnn_in['ln2_g'], 'L0_gnn_ln2_b': _L0_gnn_in['ln2_b'], 'L0_ffn_sW1': _L0_ffn_in['sW1'], 'L0_ffn_sb1': _L0_ffn_in['sb1'], 'L0_ffn_sW2': _L0_ffn_in['sW2'], 'L0_ffn_sb2': _L0_ffn_in['sb2'], 'L0_ffn_sW3': _L0_ffn_in['sW3'], 'L0_ffn_sb3': _L0_ffn_in['sb3'], 'L0_ffn_eW1': _L0_ffn_in['eW1'], 'L0_ffn_eb1': _L0_ffn_in['eb1'], 'L0_ffn_eW2': _L0_ffn_in['eW2'], 'L0_ffn_eb2': _L0_ffn_in['eb2'], 'L0_ffn_eW3': _L0_ffn_in['eW3'], 'L0_ffn_eb3': _L0_ffn_in['eb3'], 'L0_ffn_gW': _L0_ffn_in['gW'], 'L0_ffn_gb': _L0_ffn_in['gb']}

def reference(x, src, dst, L0_gnn_W_qkv, L0_gnn_W_o, L0_gnn_ln1_g, L0_gnn_ln1_b, L0_gnn_W_i, L0_gnn_W_out2, L0_gnn_ln2_g, L0_gnn_ln2_b, L0_ffn_sW1, L0_ffn_sb1, L0_ffn_sW2, L0_ffn_sb2, L0_ffn_sW3, L0_ffn_sb3, L0_ffn_eW1, L0_ffn_eb1, L0_ffn_eW2, L0_ffn_eb2, L0_ffn_eW3, L0_ffn_eb3, L0_ffn_gW, L0_ffn_gb):
    import jax
    import jax.numpy as jnp

    def _L0_gnn_ref(node_embeddings, in_graph_node_pairs, W_qkv, W_o, ln1_g, ln1_b, W_i, W_out2, ln2_g, ln2_b):
        import jax, jax.numpy as jnp
        import numpy as np
        V = 2048
        G = 32
        D = 256
        N = 8
        H = 32
        I = 1024
        LN_EPS = 1e-12

        def _layer_norm(x, g, b):
            mu = jnp.mean(x, axis=-1, keepdims=True)
            var = jnp.mean(jnp.square(x - mu), axis=-1, keepdims=True)
            return (x - mu) * jax.lax.rsqrt(var + LN_EPS) * g + b
        nV = node_embeddings.shape[0]
        src = in_graph_node_pairs[:, 0]
        dst = in_graph_node_pairs[:, 1]
        qkv = (node_embeddings @ W_qkv).reshape(nV, N, 3 * H)
        q, k, v = jnp.split(qkv, 3, axis=-1)
        scores = jnp.einsum('phi,phi->ph', q[src], k[dst]) / jnp.sqrt(jnp.float32(H))
        m = jax.ops.segment_max(scores, src, num_segments=nV)
        e = jnp.exp(scores - m[src])
        denom = jax.ops.segment_sum(e, src, num_segments=nV)
        w = e / denom[src]
        wv = w[:, :, None] * v[dst]
        att = jax.ops.segment_sum(wv, src, num_segments=nV).reshape(nV, N * H)
        pre = _layer_norm(att @ W_o + node_embeddings, ln1_g, ln1_b)
        inter = jax.nn.gelu(pre @ W_i, approximate=False)
        out = _layer_norm(inter @ W_out2 + pre, ln2_g, ln2_b)
        return out

    def _L0_ffn_ref(x, sW1, sb1, sW2, sb2, sW3, sb3, eW1, eb1, eW2, eb2, eW3, eb3, gW, gb):
        import jax, jax.numpy as jnp
        import numpy as np
        B, A = (512, 8)
        IN, OUT = (256, 256)
        SH1, SH2 = (256, 128)
        EH1, EH2 = (128, 64)
        E, TOPK = (4, 2)

        def _shared_mlp(x, W1, b1, W2, b2, W3, b3):
            h = jax.nn.relu(x @ W1 + b1)
            h = jax.nn.relu(h @ W2 + b2)
            return h @ W3 + b3

        def _experts_mlp(x, eW1, eb1, eW2, eb2, eW3, eb3):
            h = jax.nn.relu(jnp.einsum('baf,efh->ebah', x, eW1) + eb1[:, None, None, :])
            h = jax.nn.relu(jnp.einsum('ebah,ehg->ebag', h, eW2) + eb2[:, None, None, :])
            o = jnp.einsum('ebag,ego->ebao', h, eW3) + eb3[:, None, None, :]
            return jnp.moveaxis(o, 0, -1)
        all_out = _experts_mlp(x, eW1, eb1, eW2, eb2, eW3, eb3)
        shared = _shared_mlp(x, sW1, sb1, sW2, sb2, sW3, sb3)
        gates = jax.nn.softmax(x @ gW + gb, axis=-1)
        topv, topi = jax.lax.top_k(gates, TOPK)
        topw = jax.nn.softmax(topv, axis=-1)
        sel = jnp.take_along_axis(all_out, topi[:, :, None, :], axis=-1)
        gated = jnp.sum(sel * topw[:, :, None, :], axis=-1)
        return shared + gated
    edge_index_t = jnp.stack([src, dst], axis=1)
    x = x + _L0_gnn_ref(_layernorm(x, axis=-1), edge_index_t, L0_gnn_W_qkv, L0_gnn_W_o, L0_gnn_ln1_g, L0_gnn_ln1_b, L0_gnn_W_i, L0_gnn_W_out2, L0_gnn_ln2_g, L0_gnn_ln2_b)
    x = x + _L0_ffn_ref(_layernorm(x, axis=-1)[None], L0_ffn_sW1, L0_ffn_sb1, L0_ffn_sW2, L0_ffn_sb2, L0_ffn_sW3, L0_ffn_sb3, L0_ffn_eW1, L0_ffn_eb1, L0_ffn_eW2, L0_ffn_eb2, L0_ffn_eW3, L0_ffn_eb3, L0_ffn_gW, L0_ffn_gb)[0]
    return x

_drawn_inputs = setup_inputs


def setup_inputs(seed=0):
    import zlib

    import numpy as np

    out = dict(_drawn_inputs(seed))
    spreads = {'L0_gnn_ln1_g': (1.0, 0.2),
     'L0_gnn_ln1_b': (0.0, 0.1),
     'L0_gnn_ln2_g': (1.0, 0.2),
     'L0_gnn_ln2_b': (0.0, 0.1),
     'L0_ffn_sb1': (0.0, 0.782),
     'L0_ffn_sb2': (0.0, 0.377),
     'L0_ffn_sb3': (0.0, 0.1),
     'L0_ffn_eb1': (0.0, 0.8),
     'L0_ffn_eb2': (0.0, 0.8),
     'L0_ffn_eb3': (0.0, 0.1),
     'L0_ffn_gb': (0.0, 0.703)}
    factors = {'L0_gnn_W_qkv': 5.833, 'L0_gnn_W_o': 5.79}
    for name, (base, spread) in spreads.items():
        noise = np.random.default_rng([zlib.crc32(name.encode()), seed]).standard_normal(out[name].shape)
        drawn = base * np.exp(spread * noise) if base else spread * noise
        out[name] = jnp.asarray(drawn.astype(out[name].dtype))
    for name, factor in factors.items():
        out[name] = (out[name] * factor).astype(out[name].dtype)
    return out
```

```python
import concourse.bass as bass
from concourse import mybir
from contextlib import ExitStack

F32, BF16, I32 = mybir.dt.float32, mybir.dt.bfloat16, mybir.dt.int32
ALU, ACT, AX = mybir.AluOpType, mybir.ActivationFunctionType, mybir.AxisListType


class Shape:

    def __init__(s, nodes, edges, dim, heads):
        s.P = 128
        s.V, s.E, s.D, s.H = nodes, edges, dim, heads
        s.HD = dim // heads
        s.BLK = -(-nodes // s.P)
        s.TAIL = nodes - (s.BLK - 1) * s.P
        s.G = 8
        s.EC = -(-edges // s.P)
        s.EC = -(-s.EC // (4 * s.G)) * 4 * s.G
        s.GROUPS = s.EC // s.G
        s.SL = 8
        s.NB = 4
        s.MB = 8
        rows = -(-(edges + s.SL * nodes) // s.SL)
        s.RT = -(-rows // s.P)
        s.RT = -(-s.RT // s.MB) * s.MB
        s.ROWS = s.RT * s.P
        s.SLOTS = s.ROWS * s.SL
        s.NT = 2
        s.TN = max(n for n in range(1, s.P + 1) if nodes % (s.NT * n) == 0)
        s.NOWHERE = 1.0e6
        s.NEG = -1.0e30
        s.EMPTY = -1.0e20


def build_prepare(nc, S, K, x, src, dst, w_qkv):
    P, D = S.P, S.D
    with ExitStack() as ctx:
        def sb(name, shape, dt):
            return ctx.enter_context(nc.sbuf_tensor(f"prep_{name}", shape, dt))

        def pb(name, shape, dt):
            return ctx.enter_context(nc.psum_tensor(f"prep_{name}", shape, dt))

        def sem(name):
            return K.stack.enter_context(nc.semaphore(f"prep_{name}"))

        src_i = sb("src_i", [P, S.EC], I32)
        part_i = sb("part_i", [P, S.EC], I32)
        w_sb = sb("w_qkv", [P, 2, 3 * D], F32)
        xt = sb("xt", [P, 2, D], F32)
        stats = sb("stats", [P, 2, 6], F32)
        mv = sb("mv", [P, 2, 2], F32)
        std = sb("std", [P, 2, 1], F32)
        rstd = sb("rstd", [P, 2, 1], F32)
        eps = sb("eps", [P, 1], F32)
        ht = sb("ht", [P, 2, D], F32)
        hT = sb("hT", [P, 2, 2, P], F32)
        qkv = sb("qkv", [P, 2, 3 * D], F32)
        hi1 = sb("hi1", [P, 2, S.G, S.BLK], BF16)
        lo1 = sb("lo1", [P, 2, S.G, P], BF16)
        empty_slots = sb("empty_slots", [P, S.SLOTS // P], I32)
        zero_marks = sb("zero_marks", [P, S.RT], F32)

        hT_ps = pb("hT_ps", [P, 2, P], F32)
        kv_ps = pb("kv_ps", [P, 2 * D], F32)
        q_ps = pb("q_ps", [P, D], F32)
        deg_ps = pb("deg_ps", [S.BLK, P], F32)

        src_in, dst_in, w_in = sem("src_in"), sem("dst_in"), sem("w_in")
        x_in = [sem("x_in0"), sem("x_in1")]
        const, filled, tables = sem("const"), sem("filled"), sem("tables")
        lohi = sem("lohi")
        bn, mvd, sq, rs, hn = sem("bn"), sem("mvd"), sem("sq"), sem("rs"), sem("hn")
        tr, hTd, mm, kvd, qd = sem("tr"), sem("hTd"), sem("mm"), sem("kvd"), sem("qd")
        stored = [sem("stored0"), sem("stored1")]
        lo_ok, hi_ok, counted = sem("lo_ok"), sem("hi_ok"), sem("counted")
        degrees = sem("degrees")
        turns, turns_sp = sem("turns"), sem("turns_sp")

        block = ctx.enter_context(nc.Block())
        GPT = S.GROUPS // S.BLK
        assert GPT * S.BLK == S.GROUPS and GPT % 2 == 0 and S.BLK % 2 == 1

        def tiles(engine, step):
            step(0, 0, P, True)
            step(1, 1, P, True)
            with engine.Fori(1, S.BLK // 2) as i:
                step(2 * i, 0, P, False)
                step(2 * i + 1, 1, P, False)
            step(S.BLK - 1, 0, S.TAIL, False)

        @block.sync
        def _(sp):
            full = S.E // S.EC
            rest = S.E - full * S.EC
            cut = full // 16 * 16
            rows = S.E // S.EC * S.EC
            sp.wait_ge(filled, 2)
            for table, edges, done in ((src_i, src, src_in), (K.dst_i, dst, dst_in)):
                v = edges[0:rows].rearrange("(p c) -> p c", c=S.EC)
                sp.dma_start(table[0:cut, :], v[0:cut, :]).then_inc(done, 16)
                sp.dma_start(table[cut:full, :], v[cut:full, :]).then_inc(done, 16)
                sp.dma_start(table[full:full + 1, 0:rest],
                             edges[rows:S.E].rearrange("(a c) -> a c", a=1)).then_inc(done, 16)
            sp.dma_start(w_sb[:], w_qkv.rearrange("(k p) n -> p k n", p=P)).then_inc(w_in, 16)
            sp.wait_ge(filled, 4)
            sp.dma_start(K.slot_table.rearrange("(p c) o -> p (c o)", p=P), empty_slots[:]).then_inc(tables, 16)
            sp.dma_start(K.mark_table.rearrange("(p c) o -> p (c o)", p=P), zero_marks[:]).then_inc(tables, 16)

            def step(t, b, n, first):
                if not first:
                    sp.wait_ge(hn, t - 1)
                    sp.sem_inc(turns_sp, 1)
                sp.dma_start(xt[0:n, b, :], x[bass.ds(t * P, n), :]).then_inc(x_in[b], 16)
            tiles(sp, step)
            sp.wait_ge(dst_in, 48)
            sp.wait_ge(tables, 32)

        @block.gpsimd
        def _(pool):
            nc.gpsimd.memset(src_i[:], 64 * P - 1).then_inc(filled, 1)
            nc.gpsimd.memset(K.dst_i[:], 0).then_inc(filled, 1)
            nc.gpsimd.memset(empty_slots[:], S.V).then_inc(filled, 1)
            nc.gpsimd.memset(zero_marks[:], 0.0).then_inc(filled, 1)
            nc.gpsimd.iota(K.iota_i[:], pattern=[[1, P]], base=0, channel_multiplier=0).then_inc(const, 1)
            nc.gpsimd.memset(K.ident[:], 0.0).then_inc(const, 1)
            nc.gpsimd.memset(K.before[:], 1.0).then_inc(const, 1)
            nc.gpsimd.memset(K.is_node[:], 1.0).then_inc(const, 1)
            nc.gpsimd.memset(eps[:], 1e-5).then_inc(const, 1)
            pool.wait_ge(const, 5)
            nc.gpsimd.affine_select(out=K.ident[:], in_=K.ident[:], compare_op=ALU.not_equal, fill=1.0, base=0,
                                    pattern=[[-1, P]], channel_multiplier=1).then_inc(const, 1)
            nc.gpsimd.affine_select(out=K.before[:], in_=K.before[:], compare_op=ALU.is_gt, fill=0.0, base=0,
                                    pattern=[[1, P]], channel_multiplier=-1).then_inc(const, 1)
            nc.gpsimd.affine_select(out=K.is_node[:], in_=K.is_node[:], compare_op=ALU.is_gt, fill=0.0, base=S.V,
                                    pattern=[[-1, P]], channel_multiplier=-P).then_inc(const, 1)
            pool.wait_ge(const, 8)
            nc.gpsimd.tensor_copy(K.ident_b[:], K.ident[:]).then_inc(const, 1)
            nc.gpsimd.tensor_copy(K.before_b[:], K.before[:]).then_inc(const, 1)
            nc.gpsimd.tensor_copy(K.iota_b[:], K.iota_i[:]).then_inc(const, 1)
            nc.gpsimd.tensor_copy(K.iota_f[:], K.iota_i[:]).then_inc(const, 1)

        @block.vector
        def _(dve):
            dve.wait_ge(src_in, 48)
            nc.vector.tensor_single_scalar(part_i[:], src_i[:], P - 1, ALU.bitwise_and).then_inc(lohi, 1)
            dve.wait_ge(lohi, 1)
            nc.vector.tensor_copy(K.lo[:, 0:S.EC], part_i[:]).then_inc(lohi, 1)
            dve.wait_ge(lohi, 2)
            nc.vector.tensor_single_scalar(part_i[:], src_i[:], 7, ALU.arith_shift_right).then_inc(lohi, 1)
            dve.wait_ge(lohi, 3)
            nc.vector.tensor_copy(K.hi[:, 0:S.EC], part_i[:]).then_inc(lohi, 1)
            nc.vector.tensor_scalar(K.pad[:], src_i[:], float(S.V), S.NOWHERE, ALU.is_ge, ALU.mult).then_inc(lohi, 1)
            nc.vector.memset(K.lo[:, S.EC:], 0).then_inc(lohi, 1)
            nc.vector.memset(K.hi[:, S.EC:], 0).then_inc(lohi, 1)
            dve.wait_ge(lohi, 7)
            dve.wait_ge(const, 12)

            def step(t, b, n, first):
                dve.wait_ge(x_in[b], (t - b) * 8 + 16)
                nc.vector.bn_stats(stats[0:n, b, :], xt[0:n, b, :]).then_inc(bn, 1)
                dve.wait_ge(bn, t + 1)
                dve.sem_inc(turns, 1)
                nc.vector.bn_aggr(mv[0:n, b, :], stats[0:n, b, :]).then_inc(mvd, 1)
                for j in range(GPT):
                    g = GPT * t + j
                    if not (first and b == 0 and j < 2):
                        dve.wait_ge(counted, g - 1)
                    nc.vector.tensor_tensor(
                        hi1[:, j % 2], K.iota_b[:, 0:S.BLK].unsqueeze(1).to_broadcast([P, S.G, S.BLK]),
                        K.hi[:, bass.ds(g * S.G, S.G)].unsqueeze(2).to_broadcast([P, S.G, S.BLK]),
                        ALU.is_equal).then_inc(hi_ok, 1)
                    nc.vector.tensor_tensor(
                        lo1[:, j % 2], K.iota_b[:].unsqueeze(1).to_broadcast([P, S.G, P]),
                        K.lo[:, bass.ds(g * S.G, S.G)].unsqueeze(2).to_broadcast([P, S.G, P]),
                        ALU.is_equal).then_inc(lo_ok, 1)
                    if j == 1:
                        dve.wait_ge(sq, t + 1)
                        nc.vector.reciprocal(rstd[0:n, b, :], std[0:n, b, :]).then_inc(rs, 1)
                        dve.wait_ge(rs, t + 1)
                        if not first:
                            dve.wait_ge(stored[b], (t - b) * 24)
                            dve.wait_ge(tr, t - 1)
                        nc.vector.tensor_scalar(ht[0:n, b, :], xt[0:n, b, :], mv[0:n, b, 0:1], rstd[0:n, b, :],
                                                ALU.subtract, ALU.mult).then_inc(hn, 1)
                dve.wait_ge(mm, t + 1)
                if not first:
                    dve.wait_ge(stored[b], (t - b) * 24)
                nc.vector.tensor_copy(qkv[0:n, b, D:3 * D], kv_ps[0:n, :]).then_inc(kvd, 1)
            tiles(dve, step)
            dve.wait_ge(counted, S.GROUPS)
            nc.vector.tensor_copy(K.degree[:], deg_ps[:]).then_inc(degrees, 1)

        @block.scalar
        def _(act):
            act.wait_ge(const, 12)

            def step(t, b, n, first):
                act.wait_ge(mvd, t + 1)
                nc.scalar.activation(std[0:n, b, :], mv[0:n, b, 1:2], ACT.Sqrt, bias=eps[0:n, :]).then_inc(sq, 1)
                act.wait_ge(tr, t + 1)
                nc.scalar.activation(hT[:, b, :, 0:n], hT_ps[:, :, 0:n], ACT.Copy).then_inc(hTd, 1)
                act.wait_ge(mm, t + 1)
                if not first:
                    act.wait_ge(stored[b], (t - b) * 24)
                nc.scalar.activation(qkv[0:n, b, 0:D], q_ps[0:n, :], ACT.Copy,
                                     scale=float(S.HD) ** -0.5).then_inc(qd, 1)
                rows = bass.ds(t * P, n)
                act.dma_start(K.h_dram[rows, :], ht[0:n, b, :]).then_inc(stored[b], 16)
                act.wait_ge(qd, t + 1)
                act.dma_start(K.q_dram[rows, :], qkv[0:n, b, 0:D]).then_inc(stored[b], 16)
                act.wait_ge(kvd, t + 1)
                act.dma_start(K.kv_dram[rows, :], qkv[0:n, b, D:3 * D]).then_inc(stored[b], 16)
            tiles(act, step)
            act.wait_ge(stored[0], 48 * ((S.BLK + 1) // 2))
            act.wait_ge(stored[1], 48 * (S.BLK // 2))

        @block.tensor
        def _(pe):
            pe.wait_ge(w_in, 16)
            pe.wait_ge(const, 12)
            wv = w_sb[:].rearrange("p k (h c i) -> p k c h i", c=3, i=S.HD)

            def step(t, b, n, first):
                for j in range(GPT):
                    g = GPT * t + j
                    pe.wait_ge(lo_ok, g + 1)
                    pe.wait_ge(hi_ok, g + 1)
                    last_group = not first and isinstance(t, int) and j == GPT - 1
                    for c in range(S.G):
                        last = nc.tensor.matmul(deg_ps[:], hi1[:, j % 2, c, :], lo1[:, j % 2, c, :],
                                                start=(first and b == 0 and j == 0 and c == 0),
                                                stop=(last_group and c == S.G - 1), skip_group_check=True)
                    last.then_inc(counted, 1)
                    if j == 2:
                        pe.wait_ge(hn, t + 1)
                        if not (first and b == 0):
                            pe.wait_ge(hTd, t)
                        for k in range(2):
                            last = nc.tensor.transpose(hT_ps[:, k, 0:n], ht[0:n, b, k * P:(k + 1) * P],
                                                       K.ident[0:n, 0:n])
                        last.then_inc(tr, 1)
                pe.wait_ge(hTd, t + 1)
                if not (first and b == 0):
                    pe.wait_ge(kvd, t)
                    pe.wait_ge(qd, t)
                for k in range(2):
                    nc.tensor.matmul(q_ps[0:n, :], hT[:, b, k, 0:n], wv[:, k, 0], start=k == 0, stop=k == 1)
                for c in range(2):
                    for k in range(2):
                        last = nc.tensor.matmul(kv_ps[0:n, c * D:(c + 1) * D], hT[:, b, k, 0:n], wv[:, k, 1 + c],
                                                start=k == 0, stop=k == 1)
                last.then_inc(mm, 1)
            tiles(pe, step)


def build_rows(nc, S, K):
    P = S.P
    with ExitStack() as ctx:
        def sb(name, shape, dt):
            return ctx.enter_context(nc.sbuf_tensor(f"rows_{name}", shape, dt))

        def pb(name, shape, dt):
            return ctx.enter_context(nc.psum_tensor(f"rows_{name}", shape, dt))

        def sem(name):
            return K.stack.enter_context(nc.semaphore(f"rows_{name}"))

        di = sb("di", [S.BLK, P], I32)
        rows = sb("rows", [S.BLK, P], F32)
        ones = sb("ones", [P, S.RT], F32)
        upto = sb("upto", [S.BLK, P], F32)
        base = sb("base", [P, 1], F32)
        start = sb("start", [S.BLK, P], F32)
        target = sb("target", [S.BLK, P], F32)
        target_i = sb("target_i", [P, S.BLK], I32)
        mark = sb("mark", [P, S.RT], F32)
        cum = sb("cum", [P, S.RT], F32)
        node = sb("node", [P, S.RT], I32)
        flag = sb("flag", [P, S.RT], F32)
        base_ps = pb("base_ps", [P, 1], F32)
        target_ps = pb("target_ps", [P, S.BLK], F32)
        base2_ps = pb("base2_ps", [P, 1], F32)
        d, e, pm, ld, st = sem("d"), sem("e"), sem("pm"), sem("ld"), sem("st")
        sc = sem("sc")
        block = ctx.enter_context(nc.Block())

        @block.vector
        def _(dve):
            n = [0]

            def then(ins):
                n[0] += 1
                ins.then_inc(d, 1)
                dve.wait_ge(d, n[0])

            then(nc.vector.memset(ones[:], 1.0))
            then(nc.vector.tensor_single_scalar(di[:], K.degree[:], float(S.SL - 1), ALU.add))
            then(nc.vector.tensor_single_scalar(di[:], di[:], 3, ALU.arith_shift_right))
            then(nc.vector.tensor_single_scalar(rows[:], di[:], 1.0, ALU.max))
            then(nc.vector.tensor_tensor(rows[:], rows[:], K.is_node[:], ALU.mult))
            then(nc.vector.tensor_tensor_scan(upto[:], ones[0:S.BLK, 0:P], rows[:], 0.0, ALU.mult, ALU.add))
            nc.vector.tensor_tensor(start[:], upto[:], rows[:], ALU.subtract).then_inc(e, 1)
            dve.wait_ge(pm, 1)
            then(nc.vector.tensor_copy(base[0:S.BLK, :], base_ps[0:S.BLK, :]))
            dve.wait_ge(e, 1)
            then(nc.vector.tensor_scalar(start[:], start[:], base[0:S.BLK, :], None, ALU.add))
            then(nc.vector.tensor_single_scalar(K.pointer[:, 1, S.G, :], start[:], float(S.SL), ALU.mult))
            then(nc.vector.tensor_scalar(target[:], K.is_node[:], -S.NOWHERE, S.NOWHERE, ALU.mult, ALU.add))
            nc.vector.tensor_tensor(target[:], target[:], start[:], ALU.add).then_inc(e, 1)
            dve.wait_ge(pm, 2)
            nc.vector.tensor_copy(target_i[:], target_ps[:]).then_inc(e, 1)
            dve.wait_ge(ld, 16)
            then(nc.vector.tensor_tensor_scan(cum[:], ones[:], mark[:], 0.0, ALU.mult, ALU.add))
            nc.vector.tensor_single_scalar(flag[:], mark[:], S.NEG, ALU.mult).then_inc(e, 1)
            dve.wait_ge(pm, 3)
            then(nc.vector.tensor_copy(base[:], base2_ps[:]))
            nc.vector.tensor_scalar(node[:], cum[:], base[:], -1.0, ALU.add, ALU.add).then_inc(e, 1)

        @block.tensor
        def _(pe):
            pe.wait_ge(e, 1)
            nc.tensor.matmul(base_ps[0:S.BLK, :], K.before[0:S.BLK, 0:S.BLK], upto[:, P - 1:P],
                             start=True, stop=True).then_inc(pm, 1)
            pe.wait_ge(e, 2)
            nc.tensor.transpose(target_ps[:], target[:], K.ident[0:S.BLK, 0:S.BLK]).then_inc(pm, 1)
            pe.wait_ge(e, 4)
            nc.tensor.matmul(base2_ps[:], K.before[:], cum[:, S.RT - 1:S.RT], start=True, stop=True).then_inc(pm, 1)

        @block.gpsimd
        def _(pool):
            pool.wait_ge(e, 3)
            pool.wait_ge(d, 1)
            for c in range(S.BLK):
                pool.indirect_dma_start(
                    out=K.mark_table, out_offset=bass.IndirectOffsetOnAxis(ap=target_i[:, c:c + 1], axis=0),
                    in_=ones[:, 0:1], in_offset=None, bounds_check=S.ROWS - 1, oob_is_err=False).then_inc(sc, 16)
            pool.wait_ge(sc, 16 * S.BLK)

        @block.sync
        def _(sp):
            sp.wait_ge(sc, 16 * S.BLK)
            sp.dma_start(mark[:], K.mark_table.rearrange("(p c) o -> p (c o)", p=P)).then_inc(ld, 16)
            sp.wait_ge(e, 4)
            sp.dma_start(K.flag_table[0:S.ROWS].rearrange("(p c) -> p c", p=P), flag[:]).then_inc(st, 16)
            sp.dma_start(K.flag_table[S.ROWS:S.ROWS + 1].rearrange("(p c) -> p c", p=1),
                         flag[0:1, 0:1]).then_inc(st, 16)
            sp.wait_ge(e, 5)
            sp.dma_start(K.node_table.rearrange("(p c) -> p c", p=P), node[:]).then_inc(st, 16)
            sp.wait_ge(st, 48)


def build_slots(nc, S, K):
    P, G, HALF = S.P, S.G, S.G // 2
    with ExitStack() as ctx:
        def sb(name, shape, dt):
            return ctx.enter_context(nc.sbuf_tensor(f"slots_{name}", shape, dt))

        def pb(name, shape, dt):
            return ctx.enter_context(nc.psum_tensor(f"slots_{name}", shape, dt))

        def sem(name):
            return K.stack.enter_context(nc.semaphore(f"slots_{name}"))

        hi1 = sb("hi1", [P, 2, G, S.BLK], BF16)
        lo1 = sb("lo1", [P, 2, G, P], BF16)
        hiT_b = sb("hiT_b", [S.BLK, G, P], BF16)
        hiT_f = sb("hiT_f", [S.BLK, G, P], F32)
        same = sb("same", [P, G, P], BF16)
        picked = sb("picked", [P, G, P], F32)
        slot_f = sb("slot_f", [P, 2, G], F32)
        slot_i = sb("slot_i", [P, 2, G], I32)
        dst_s = sb("dst_s", [P, 2, G], I32)
        hiT_ps = [pb(f"hiT_ps{h}", [S.BLK, HALF, P], BF16) for h in range(2)]
        same_ps = [pb(f"same_ps{h}", [P, HALF, P], F32) for h in range(2)]
        run_ps = [pb(f"run_ps{h}", [S.BLK, HALF, P], F32) for h in range(2)]
        at_ps = [pb(f"at_ps{h}", [P, HALF, P], F32) for h in range(2)]

        onehots = sem("onehots")
        turned = sem("turned")
        hiT_ok = sem("hiT_ok")
        grams = sem("grams")
        runs = sem("runs")
        masked = sem("masked")
        moved = sem("moved")
        looked = sem("looked")
        picks = sem("picks")
        slots = sem("slots")
        dsts = sem("dsts")
        scattered = [sem("scattered0"), sem("scattered1")]
        turns, turns_pe = sem("turns"), sem("turns_pe")
        block = ctx.enter_context(nc.Block())

        def groups(engine, step):
            step(0, 0, True)
            step(1, 1, True)
            with engine.Fori(1, S.GROUPS // 2) as i:
                step(2 * i, 0, False)
                step(2 * i + 1, 1, False)

        @block.vector
        def _(dve):
            def one_hots(g, b, first, col):
                if not first:
                    dve.wait_ge(looked, 2 * g - 2)
                nc.vector.tensor_tensor(
                    hi1[:, b], K.iota_b[:, 0:S.BLK].unsqueeze(1).to_broadcast([P, G, S.BLK]),
                    K.hi[:, col].unsqueeze(2).to_broadcast([P, G, S.BLK]), ALU.is_equal).then_inc(onehots, 1)
                nc.vector.tensor_tensor(
                    lo1[:, b], K.iota_b[:].unsqueeze(1).to_broadcast([P, G, P]),
                    K.lo[:, col].unsqueeze(2).to_broadcast([P, G, P]), ALU.is_equal).then_inc(onehots, 1)

            one_hots(0, 0, True, slice(0, G))

            def step(g, b, first):
                for h in range(2):
                    dve.wait_ge(runs, 2 * g + h + 1)
                    if not (first and b == 0 and h == 0):
                        dve.wait_ge(moved, 2 * g + h)
                    if not first or (b and h):
                        dve.wait_ge(looked, 2 * g - 2 + h)
                    before = K.pointer[:, b, HALF, :] if h else K.pointer[:, 1 - b, G, :]
                    nc.vector.tensor_tensor(K.pointer[:, b, 1 + h * HALF:1 + (h + 1) * HALF, :], run_ps[h][:],
                                            before.unsqueeze(1).to_broadcast([S.BLK, HALF, P]),
                                            ALU.add).then_inc(moved, 1)
                for h in range(2):
                    dve.wait_ge(grams, 2 * g + h + 1)
                    if not (first and b == 0):
                        dve.wait_ge(looked, 2 * g - 1 + h)
                    nc.vector.tensor_tensor(same[:, h * HALF:(h + 1) * HALF, :], same_ps[h][:],
                                            K.before_b[:].unsqueeze(1).to_broadcast([P, HALF, P]),
                                            ALU.mult).then_inc(masked, 1)
                one_hots(g + 1, 1 - b, first and b == 0, bass.ds((g + 1) * G, G))
                for c in range(G):
                    dve.wait_ge(looked, 2 * g + 1 + c // HALF)
                    if not first and c == 0:
                        dve.wait_ge(slots, g - 1)
                    nc.vector.tensor_tensor_reduce(out=picked[:, c, :], in0=at_ps[c // HALF][:, c % HALF, :],
                                                   in1=lo1[:, b, c, :], scale=1.0, scalar=0.0, op0=ALU.mult,
                                                   op1=ALU.add, accum_out=slot_f[:, b, c:c + 1]).then_inc(picks, 1)
                dve.wait_ge(picks, G * g + G)
                if not first:
                    dve.wait_ge(scattered[b], (g - b) * 8 * G)
                nc.vector.tensor_tensor(slot_i[:, b, :], slot_f[:, b, :], K.pad[:, bass.ds(g * G, G)],
                                        ALU.add).then_inc(slots, 1)
            groups(dve, step)

        @block.tensor
        def _(pe):
            def ahead(g, b, first):
                pe.wait_ge(onehots, 2 * g + 2)
                for h in range(2):
                    if not first:
                        pe.wait_ge(hiT_ok, 4 * g - 2 + 2 * h)
                    pe.sem_inc(turns_pe, 1)
                    for c in range(HALF):
                        last = nc.tensor.transpose(hiT_ps[h][:, c, :], hi1[:, b, h * HALF + c, :], K.ident_b[:])
                    last.then_inc(turned, 1)
                for h in range(2):
                    if not first:
                        pe.wait_ge(moved, 2 * g - 1 + h)
                    for c in range(HALF):
                        for k in range(c + 1):
                            last = nc.tensor.matmul(run_ps[h][:, c, :], hi1[:, b, h * HALF + k, :],
                                                    lo1[:, b, h * HALF + k, :], start=k == 0, stop=k == c)
                    last.then_inc(runs, 1)
                for h in range(2):
                    pe.wait_ge(hiT_ok, 4 * g + 2 + 2 * h)
                    if not first:
                        pe.wait_ge(masked, 2 * g - 1 + h)
                    for c in range(HALF):
                        v = hiT_b[:, h * HALF + c, :]
                        last = nc.tensor.matmul(same_ps[h][:, c, :], v, v, start=True, stop=True)
                    last.then_inc(grams, 1)

            def look(g, b, first):
                for h in range(2):
                    pe.wait_ge(moved, 2 * g + h + 1)
                    pe.wait_ge(masked, 2 * g + h + 1)
                    if not (first and b == 0):
                        pe.wait_ge(picks, G * g - HALF + h * HALF)
                    for c in range(HALF):
                        k = h * HALF + c
                        pointer = K.pointer[:, b, k, :] if k else K.pointer[:, 1 - b, G, :]
                        nc.tensor.matmul(at_ps[h][:, c, :], hiT_f[:, k, :], pointer, start=True, stop=False)
                        last = nc.tensor.matmul(at_ps[h][:, c, :], same[:, k, :], lo1[:, b, k, :],
                                                start=False, stop=True)
                    last.then_inc(looked, 1)

            ahead(0, 0, True)
            look(0, 0, True)
            ahead(1, 1, False)
            look(1, 1, True)
            with pe.Fori(1, S.GROUPS // 2) as i:
                ahead(2 * i, 0, False)
                look(2 * i, 0, False)
                ahead(2 * i + 1, 1, False)
                look(2 * i + 1, 1, False)

        @block.scalar
        def _(act):
            def step(g, b, first):
                for h in range(2):
                    part = slice(h * HALF, (h + 1) * HALF)
                    act.wait_ge(turned, 2 * g + h + 1)
                    if not (first and b == 0):
                        act.wait_ge(looked, 2 * g - 1 + h)
                    nc.scalar.activation(hiT_b[:, part, :], hiT_ps[h][:], ACT.Copy).then_inc(hiT_ok, 1)
                    nc.scalar.activation(hiT_f[:, part, :], hiT_ps[h][:], ACT.Copy).then_inc(hiT_ok, 1)
                if not first:
                    act.wait_ge(scattered[b], (g - b) * 8 * G)
                nc.scalar.activation(dst_s[:, b, :], K.dst_i[:, bass.ds(g * G, G)], ACT.Copy).then_inc(dsts, 1)
            groups(act, step)

        @block.gpsimd
        def _(pool):
            def step(g, b, first):
                pool.wait_ge(slots, g + 1)
                pool.wait_ge(dsts, g + 1)
                pool.sem_inc(turns, 1)
                for c in range(G):
                    pool.indirect_dma_start(
                        out=K.slot_table, out_offset=bass.IndirectOffsetOnAxis(ap=slot_i[:, b, c:c + 1], axis=0),
                        in_=dst_s[:, b, c:c + 1], in_offset=None, bounds_check=S.SLOTS - 1,
                        oob_is_err=False).then_inc(scattered[b], 16)
            groups(pool, step)
            pool.wait_ge(scattered[0], 8 * G * S.GROUPS)
            pool.wait_ge(scattered[1], 8 * G * S.GROUPS)


def build_attention(nc, S, K):
    P, D, H, SL, NB, MB, T = S.P, S.D, S.H, S.SL, S.NB, S.MB, S.RT
    GATHERS = 16 * (SL + 1)
    with ExitStack() as ctx:
        def sb(name, shape, dt):
            return ctx.enter_context(nc.sbuf_tensor(f"att_{name}", shape, dt))

        def pb(name, shape, dt):
            return ctx.enter_context(nc.psum_tensor(f"att_{name}", shape, dt))

        def sem(name):
            return K.stack.enter_context(nc.semaphore(f"att_{name}"))

        idx = sb("idx", [P, MB, SL], I32)
        node = sb("node", [P, MB], I32)
        first_node = sb("first_node", [P, MB], I32)
        flags = sb("flags", [H, MB, P + 1], F32)
        kv = [sb(f"kv{b}", [P, SL, 2 * D], F32) for b in range(NB)]
        q = [sb(f"q{b}", [P, D], F32) for b in range(NB)]
        prod = sb("prod", [P, SL, D], F32)
        ev = [sb(f"ev{k}", [P, SL, D], F32) for k in range(2)]
        local = sb("local", [P, NB], F32)
        onehot = sb("onehot", [P, NB, P], F32)
        absent = sb("absent", [P, SL], F32)
        raw = sb("raw", [P, SL, H], F32)
        score = sb("score", [P, NB, SL, H], F32)
        rawmax = sb("rawmax", [P, H], F32)
        rowmax = sb("rowmax", [P, NB, H], F32)
        upto = sb("upto", [H, NB, P], F32)
        top = sb("top", [H, NB, P], F32)
        drop = sb("drop", [H, NB], F32)
        shifted = sb("shifted", [P, NB, SL, H], F32)
        e = sb("e", [P, NB, SL, H], F32)
        esum = sb("esum", [P, NB, H], F32)
        fade = sb("fade", [H, NB], F32)
        fadeT = sb("fadeT", [P, NB, 2], F32)
        new_att = sb("new_att", [P, 2], F32)
        new_den = sb("new_den", [H, 1], F32)

        maxT_ps = pb("maxT_ps", [H, P], F32)
        top_ps = pb("top_ps", [P, H], F32)
        fade_ps = pb("fade_ps", [P, 2], F32)
        att_ps = [pb(f"att_ps{k}", [P, 2, P], F32) for k in range(2)]
        den_ps = [pb(f"den_ps{k}", [H, P], F32) for k in range(2)]

        tabled = [sem(f"tabled{m}") for m in range(MB)]
        gathered = [sem(f"gathered{b}") for b in range(NB)]
        prep = sem("prep")
        turns, turns_pe, turns_sp = sem("turns"), sem("turns_pe"), sem("turns_sp")
        multiplied = sem("multiplied")
        reduced = sem("reduced")
        absents = sem("absents")
        scored = sem("scored")
        rawmaxed = sem("rawmaxed")
        maxed = sem("maxed")
        maxT = sem("maxT")
        scanned = sem("scanned")
        dropped = sem("dropped")
        topped = sem("topped")
        shifts = sem("shifts")
        exps = sem("exps")
        esums = sem("esums")
        weighted = sem("weighted")
        locals_ = sem("locals")
        hot = sem("hot")
        fades = sem("fades")
        spread = sem("spread")
        fadesT = sem("fadesT")
        summed = sem("summed")
        columns = sem("columns")
        placed = sem("placed")
        block = ctx.enter_context(nc.Block())

        def tiles(engine, step):
            for u in range(MB):
                step(0, u)
            with engine.Fori(1, T // MB) as i:
                for u in range(MB):
                    step(i, u)

        def before(i, u):
            return (i, u - 1) if u else (i - 1, MB - 1)

        def turn(i, u):
            return i * (MB // NB) + u // NB

        def starts(i, u):
            return isinstance(i, int) and i == 0 and u == 0

        def has(i, u, back):
            return not isinstance(i, int) or MB * i + u >= back

        @block.sync
        def _(sp):
            def step(i, u):
                t = MB * i + u
                if has(i, u, MB):
                    sp.wait_ge(placed, 4 * (t - MB + 1))
                    sp.sem_inc(turns_sp, 1)
                    sp.wait_ge(gathered[u % NB], GATHERS * (turn(i, u) - MB // NB + 1))
                    sp.sem_inc(turns_sp, 1)
                sp.dma_start(idx[:, u, :],
                             K.slot_table[bass.ds(t * (P * SL), P * SL)].rearrange("(p c) o -> p (c o)", p=P))\
                  .then_inc(tabled[u], 16)
                sp.dma_start(node[:, u:u + 1], K.node_table[bass.ds(t * P, P)].rearrange("(p o) -> p o", o=1))\
                  .then_inc(tabled[u], 16)
                sp.dma_start(first_node[:, u:u + 1],
                             K.node_table[bass.ds(t * P, 1)].rearrange("(p o) -> p o", o=1).to_broadcast([P, 1]))\
                  .then_inc(tabled[u], 16)
                sp.dma_start(flags[:, u, :],
                             K.flag_table[bass.ds(t * P, P + 1)].rearrange("(o c) -> o c", o=1).to_broadcast([H, P + 1]))\
                  .then_inc(tabled[u], 16)
            tiles(sp, step)

        @block.gpsimd
        def _(pool):
            for b in range(NB):
                nc.gpsimd.memset(kv[b][:], 0.0).then_inc(prep, 1)
            nc.gpsimd.memset(upto[:, NB - 1, P - 1:P], S.EMPTY).then_inc(prep, 1)
            nc.gpsimd.memset(K.attT[:], 0.0).then_inc(prep, 1)
            nc.gpsimd.memset(K.denT[:], 0.0).then_inc(prep, 1)
            sp3 = K.spreader[:].rearrange("h (a b) -> h a b", b=S.HD)
            nc.gpsimd.memset(K.spreader[:], 0.0).then_inc(prep, 1)
            pool.wait_ge(prep, NB + 4)
            nc.gpsimd.affine_select(out=sp3, in_=sp3, compare_op=ALU.not_equal, fill=1.0, base=0,
                                    pattern=[[-1, H], [0, S.HD]], channel_multiplier=1).then_inc(prep, 1)

            def step(i, u):
                t, b = MB * i + u, u % NB
                pool.wait_ge(tabled[u], 64 * (i + 1))
                if has(i, u, NB):
                    pool.wait_ge(weighted, t - NB + 1)
                pool.sem_inc(turns, 1)
                pool.indirect_dma_start(
                    out=q[b][:], out_offset=None, in_=K.q_dram,
                    in_offset=bass.IndirectOffsetOnAxis(ap=node[:, u:u + 1], axis=0),
                    bounds_check=S.V - 1, oob_is_err=False).then_inc(gathered[b], 16)
                for j in range(SL):
                    pool.indirect_dma_start(
                        out=kv[b][:, j, :], out_offset=None, in_=K.kv_dram,
                        in_offset=bass.IndirectOffsetOnAxis(ap=idx[:, u, j:j + 1], axis=0),
                        bounds_check=S.V - 1, oob_is_err=False).then_inc(gathered[b], 16)
            tiles(pool, step)

        @block.vector
        def _(dve):
            dve.wait_ge(prep, NB + 5)

            def shift(i, u):
                t, b = MB * i + u, u % NB
                dve.wait_ge(topped, t + 1)
                if has(i, u, NB):
                    dve.wait_ge(exps, t - NB + 1)
                nc.vector.tensor_tensor(shifted[:, b], score[:, b], top_ps[:].unsqueeze(1).to_broadcast([P, SL, H]),
                                        ALU.subtract).then_inc(shifts, 1)

            def weigh(i, u):
                t, b = MB * i + u, u % NB
                if has(i, u, 2):
                    dve.wait_ge(summed, t - 1)
                nc.vector.tensor_tensor(ev[u % 2][:].rearrange("p s (h c) -> p s h c", h=H),
                                        kv[b][:, :, D:2 * D].rearrange("p s (h c) -> p s h c", h=H),
                                        e[:, b].unsqueeze(3).to_broadcast([P, SL, H, S.HD]),
                                        ALU.mult).then_inc(weighted, 1)

            def sums(i, u):
                t, b = MB * i + u, u % NB
                dve.wait_ge(exps, t + 1)
                nc.vector.tensor_reduce(esum[:, b, :], e[:, b].rearrange("p s h -> p h s"), AX.X, ALU.add)\
                    .then_inc(esums, 1)

            def step(i, u):
                t, b = MB * i + u, u % NB
                pb_, pi, pu = (u - 1) % NB, *before(i, u)
                dve.wait_ge(gathered[b], GATHERS * (turn(i, u) + 1))
                if not starts(i, u):
                    dve.wait_ge(reduced, t)
                nc.vector.tensor_tensor(prod[:], kv[b][:, :, 0:D], q[b][:].unsqueeze(1).to_broadcast([P, SL, D]),
                                        ALU.mult).then_inc(multiplied, 1)
                if not starts(i, u):
                    shift(pi, pu)
                dve.wait_ge(multiplied, t + 1)
                if not starts(i, u):
                    dve.wait_ge(scored, t)
                nc.vector.tensor_reduce(raw[:].rearrange("p s h -> p (s h)"),
                                        prod[:].rearrange("p s (h c) -> p (s h) c", h=H), AX.X, ALU.add)\
                    .then_inc(reduced, 1)
                nc.vector.tensor_scalar(absent[:], idx[:, u, :], float(S.V), S.NEG, ALU.is_ge, ALU.mult)\
                    .then_inc(absents, 1)
                dve.wait_ge(reduced, t + 1)
                dve.wait_ge(absents, t + 1)
                nc.vector.tensor_tensor(score[:, b], raw[:], absent[:].unsqueeze(2).to_broadcast([P, SL, H]),
                                        ALU.add).then_inc(scored, 1)
                dve.wait_ge(scored, t + 1)
                nc.vector.tensor_reduce(rawmax[:], score[:, b].rearrange("p s h -> p h s"), AX.X, ALU.max)\
                    .then_inc(rawmaxed, 1)
                dve.wait_ge(rawmaxed, t + 1)
                nc.vector.tensor_single_scalar(rowmax[:, b, :], rawmax[:], S.EMPTY, ALU.max).then_inc(maxed, 1)
                nc.vector.tensor_tensor(local[:, b:b + 1], node[:, u:u + 1], first_node[:, u:u + 1],
                                        ALU.subtract).then_inc(locals_, 1)
                if not starts(i, u):
                    sums(pi, pu)
                dve.wait_ge(locals_, t + 1)
                if has(i, u, NB):
                    dve.wait_ge(summed, t - NB + 1)
                nc.vector.tensor_scalar(onehot[:, b, :], K.iota_f[:], local[:, b:b + 1], None, ALU.is_equal)\
                    .then_inc(hot, 1)
                dve.wait_ge(maxT, t + 1)
                if not starts(i, u):
                    dve.wait_ge(scanned, 2 * t)
                nc.vector.tensor_tensor_scan(upto[:, b, :], flags[:, u, 0:P], maxT_ps[:], upto[:, pb_, P - 1:P],
                                             ALU.add, ALU.max).then_inc(scanned, 1)
                dve.wait_ge(scanned, 2 * t + 1)
                nc.vector.tensor_tensor_scan(top[:, b, ::-1], flags[:, u, P:0:-1], upto[:, b, ::-1], S.NEG,
                                             ALU.add, ALU.max).then_inc(scanned, 1)
                dve.wait_ge(scanned, 2 * t + 2)
                nc.vector.scalar_tensor_tensor(out=drop[:, b:b + 1], in0=upto[:, pb_, P - 1:P],
                                               scalar=flags[:, u, 0:1], in1=top[:, b, 0:1], op0=ALU.add,
                                               op1=ALU.subtract).then_inc(dropped, 1)
                if not starts(i, u):
                    weigh(pi, pu)
            tiles(dve, step)
            last = (T // MB - 1, MB - 1)
            shift(*last)
            sums(*last)
            weigh(*last)

        @block.tensor
        def _(pe):
            pe.wait_ge(prep, NB + 5)

            def attend(i, u, k):
                t, b = MB * i + u, u % NB
                if k == 0:
                    pe.wait_ge(weighted, t + 1)
                    if has(i, u, 2):
                        pe.wait_ge(placed, 4 * t - 4)
                for j in range(SL):
                    nc.tensor.matmul(att_ps[u % 2][:, k, :], ev[u % 2][:, j, k * P:(k + 1) * P], onehot[:, b, :],
                                     start=j == 0, stop=j == SL - 1)
                if k == 1:
                    nc.tensor.matmul(den_ps[u % 2][:], esum[:, b, :], onehot[:, b, :], start=True, stop=True)\
                        .then_inc(summed, 1)

            def step(i, u):
                t, b = MB * i + u, u % NB
                if has(i, u, 2):
                    attend(*before(*before(i, u)), 0)
                pe.wait_ge(maxed, t + 1)
                if not starts(i, u):
                    pe.wait_ge(scanned, 2 * t)
                nc.tensor.transpose(maxT_ps[:], rowmax[:, b, :], K.ident[:]).then_inc(maxT, 1)
                pe.wait_ge(scanned, 2 * t + 2)
                if not starts(i, u):
                    pe.wait_ge(shifts, t)
                pe.sem_inc(turns_pe, 1)
                nc.tensor.transpose(top_ps[:], top[:, b, :], K.ident[0:H, 0:H]).then_inc(topped, 1)
                pe.wait_ge(fades, t + 1)
                if not starts(i, u):
                    pe.wait_ge(fadesT, t)
                for k in range(2):
                    last = nc.tensor.matmul(fade_ps[:, k:k + 1], K.spreader[:, k * P:(k + 1) * P], fade[:, b:b + 1],
                                            start=True, stop=True)
                last.then_inc(spread, 1)
                if has(i, u, 2):
                    attend(*before(*before(i, u)), 1)
            tiles(pe, step)
            for u in (MB - 2, MB - 1):
                for k in range(2):
                    attend(T // MB - 1, u, k)

        @block.scalar
        def _(act):
            act.wait_ge(prep, NB + 5)

            def exponentials(i, u):
                t, b = MB * i + u, u % NB
                act.wait_ge(shifts, t + 1)
                if has(i, u, NB):
                    act.wait_ge(weighted, t - NB + 1)
                nc.scalar.activation(e[:, b], shifted[:, b], ACT.Exp).then_inc(exps, 1)

            def place(i, u):
                t, b = MB * i + u, u % NB
                n0 = act.value_load(first_node[0:1, u:u + 1], min_val=0, max_val=S.V)
                act.wait_ge(summed, t + 1)
                nc.scalar.activation(new_att[:], att_ps[u % 2][:, :, 0], ACT.Copy).then_inc(columns, 1)
                nc.scalar.activation(new_den[:], den_ps[u % 2][:, 0:1], ACT.Copy).then_inc(columns, 1)
                nc.scalar.activation(K.attT[:, :, bass.ds(n0 + 1, P - 1)], att_ps[u % 2][:, :, 1:P], ACT.Copy)
                nc.scalar.activation(K.denT[:, bass.ds(n0 + 1, P - 1)], den_ps[u % 2][:, 1:P], ACT.Copy).then_inc(placed, 1)
                act.wait_ge(columns, 2 * t + 2)
                for k in range(2):
                    nc.scalar.activation(K.attT[:, k, bass.ds(n0, 1)], K.attT[:, k, bass.ds(n0, 1)], ACT.Identity,
                                         bias=new_att[:, k:k + 1], scale=fadeT[:, b, k:k + 1]).then_inc(placed, 1)
                nc.scalar.activation(K.denT[:, bass.ds(n0, 1)], K.denT[:, bass.ds(n0, 1)], ACT.Identity,
                                     bias=new_den[:], scale=fade[:, b:b + 1]).then_inc(placed, 1)
                act.wait_ge(placed, 4 * t + 4)

            def step(i, u):
                t, b = MB * i + u, u % NB
                if not starts(i, u):
                    exponentials(*before(i, u))
                act.wait_ge(dropped, t + 1)
                nc.scalar.activation(fade[:, b:b + 1], drop[:, b:b + 1], ACT.Exp).then_inc(fades, 1)
                act.wait_ge(spread, t + 1)
                nc.scalar.activation(fadeT[:, b, :], fade_ps[:], ACT.Copy).then_inc(fadesT, 1)
                if has(i, u, 2):
                    place(*before(*before(i, u)))
            tiles(act, step)
            exponentials(T // MB - 1, MB - 1)
            place(T // MB - 1, MB - 2)
            place(T // MB - 1, MB - 1)


def build_dense(nc, S, K, A, out):
    P, D, H = S.P, S.D, S.H
    TN, NT = S.TN, S.NT
    N = TN * NT
    GR = S.V // N
    FF = A.w_i.shape[1]
    FC = FF // P
    NE, E1, E2 = A.e_w1.shape[0], A.e_w1.shape[2], A.e_w2.shape[2]
    M1, M2 = A.s_w1.shape[1], A.s_w2.shape[1]
    assert GR * N == S.V and GR % 2 == 1 and E1 == P and M2 == P and M1 == 2 * P and D == 2 * P
    with ExitStack() as ctx:
        def sb(name, shape, dt):
            return ctx.enter_context(nc.sbuf_tensor(f"mlp_{name}", shape, dt))

        def pb(name, shape, dt):
            return ctx.enter_context(nc.psum_tensor(f"mlp_{name}", shape, dt))

        def sem(name):
            return K.stack.enter_context(nc.semaphore(f"mlp_{name}"))

        w_o = sb("w_o", [P, 2, D], F32)
        w_i = sb("w_i", [P, 2, FF], F32)
        w_2 = sb("w_2", [P, FC, D], F32)
        s_w1 = sb("s_w1", [P, 2, M1], F32)
        s_w2 = sb("s_w2", [P, 2, M2], F32)
        s_w3 = sb("s_w3", [P, D], F32)
        e_w1 = sb("e_w1", [P, NE, 2, E1], F32)
        e_w2 = sb("e_w2", [P, NE, E2], F32)
        e_w3 = sb("e_w3", [E2 + 1, NE, D], F32)
        g_w = sb("g_w", [P, 2, NE], F32)
        s_b1 = sb("s_b1", [P, 2], F32)
        s_b2 = sb("s_b2", [P, 1], F32)
        s_b3 = sb("s_b3", [1, D], F32)
        e_b1 = sb("e_b1", [P, NE], F32)
        e_b2 = sb("e_b2", [E2, NE], F32)
        g_b = sb("g_b", [P, NE], F32)
        gains = sb("gains", [P, 4, D], F32)
        ones = sb("ones", [1, P], F32)
        minus_half = sb("minus_half", [P, NT], F32)
        earlier = sb("earlier", [P, NE, NE], F32)

        h = sb("h", [TN, 2, NT, D], F32)
        xr = sb("xr", [TN, 2, NT, D], F32)
        attn = sb("attn", [P, 2, N], F32)
        z = sb("z", [TN, NT, D], F32)
        stats = sb("stats", [TN, NT, 6], F32)
        mv = sb("mv", [TN, NT, 2], F32)
        var = sb("var", [TN, NT], F32)
        rstd = sb("rstd", [TN, NT], F32)
        pre = sb("pre", [TN, 2, NT, D], F32)
        preT = sb("preT", [P, 2, N], F32)
        inter = sb("inter", [P, FC, N], F32)
        z2 = sb("z2", [TN, NT, D], F32)
        x1 = sb("x1", [TN, 2, NT, D], F32)
        xn = sb("xn", [TN, 2, NT, D], F32)
        xnT = sb("xnT", [P, 2, N], F32)
        h1 = sb("h1", [P, 2, N], F32)
        h2 = sb("h2", [P, N], F32)
        a1 = sb("a1", [P, NE, N], F32)
        a2 = sb("a2", [E2 + 1, NE, N], F32)
        lg = sb("lg", [TN, NT, NE], F32)
        g1 = sb("g1", [TN, NT], F32)
        g2 = sb("g2", [TN, NT, NE], F32)
        g3 = sb("g3", [TN, NT, NE], F32)
        pg = sb("pg", [TN, NT, NE], F32)
        beats = sb("beats", [TN, NT, NE, NE], F32)
        ties = sb("ties", [TN, NT, NE, NE], F32)
        wt = sb("wt", [TN, NT, NE], F32)
        res = sb("res", [TN, 2, NT, D], F32)

        den_ps = pb("den_ps", [P, 2, N], F32)
        ya_ps = pb("ya_ps", [TN, NT, D], F32)
        yb_ps = pb("yb_ps", [TN, NT, D], F32)
        tr_ps = pb("tr_ps", [P, 2, N], F32)
        mm_ps = [pb(f"mm_ps{i}", [P, 2, N], F32) for i in range(2)]
        o_ps = [pb(f"o_ps{i}", [TN, 2, D], F32) for i in range(2)]

        weights, bias_in, consts, rden = sem("weights"), sem("bias_in"), sem("consts"), sem("rden")
        in_h = [sem("in_h0"), sem("in_h1")]
        in_x = [sem("in_x0"), sem("in_x1")]
        out_done = [sem("out_done0"), sem("out_done1")]
        turns, turns_pe, turns_pool = sem("turns"), sem("turns_pe"), sem("turns_pool")
        spread = sem("spread")
        normed = sem("normed")
        projected = sem("projected")
        zs = sem("zs")
        step_v = sem("step_v")
        vars_ = sem("vars")
        rstds = sem("rstds")
        pres = sem("pres")
        preTs = sem("preTs")
        copied = sem("copied")
        mms = sem("mms")
        acts = sem("acts")
        downs = sem("downs")
        x1s = sem("x1s")
        xns = sem("xns")
        logits = sem("logits")
        lgs = sem("lgs")
        ex_in, ex_out = sem("ex_in"), sem("ex_out")
        outs = sem("outs")
        used = sem("used")
        results = sem("results")
        block = ctx.enter_context(nc.Block())

        FM = FC // 2
        EM = 1 + 1 + 2 + 2
        MM = FM + EM

        def groups(engine, step):
            step(0, 0, True, False)
            step(1, 1, True, True)
            step(2, 0, True, True)
            with engine.Fori(1, (GR - 3) // 2) as i:
                step(2 * i + 1, 1, True, True)
                step(2 * i + 2, 0, True, True)
            step(GR - 2, 1, True, True)
            step(GR - 1, 0, False, True)
            step(GR, 1, False, True)

        def is_int(g, n):
            return isinstance(g, int) and g == n

        def mm_base(g, second):
            if second:
                return (g + 2) * FM + g * EM if not is_int(g, GR - 1) else GR * FM + (GR - 1) * EM
            return g * FM + (g - 1) * EM if not is_int(g, 0) else 0

        @block.sync
        def _(sp):
            def load(dst, src_):
                sp.dma_start(dst, src_).then_inc(weights, 16)

            load(w_o[:], A.w_o.rearrange("(k p) n -> p k n", p=P))
            load(w_i[:], A.w_i.rearrange("(k p) n -> p k n", p=P))
            load(w_2[:], A.w_out2.rearrange("(k p) n -> p k n", p=P))
            load(s_w1[:], A.s_w1.rearrange("(k p) n -> p k n", p=P))
            load(s_w2[:], A.s_w2.rearrange("(k p) n -> p k n", p=P))
            load(s_w3[:], A.s_w3)
            for e in range(NE):
                load(e_w1[:, e], A.e_w1[e].rearrange("(k p) n -> p k n", p=P))
                load(e_w2[:, e], A.e_w2[e])
                load(e_w3[0:E2, e], A.e_w3[e])
                load(e_b1[:, e:e + 1], A.e_b1[e].rearrange("(p o) -> p o", o=1))
                load(e_b2[:, e:e + 1], A.e_b2[e].rearrange("(p o) -> p o", o=1))
            load(e_w3[E2:E2 + 1], A.e_b3.rearrange("(o e) n -> o e n", o=1))
            load(g_w[:], A.g_w.rearrange("(k p) n -> p k n", p=P))
            for k in range(2):
                load(s_b1[:, k:k + 1], A.s_b1[k * P:(k + 1) * P].rearrange("(p o) -> p o", o=1))
            load(s_b2[:], A.s_b2.rearrange("(p o) -> p o", o=1))
            load(s_b3[:], A.s_b3.rearrange("(o n) -> o n", o=1))
            load(g_b[:], A.g_b.rearrange("(o n) -> o n", o=1).to_broadcast([P, NE]))
            for i, v in enumerate((A.ln1_g, A.ln1_b, A.ln2_g, A.ln2_b)):
                load(gains[:, i, :], v.rearrange("(o n) -> o n", o=1).to_broadcast([P, D]))

            def fetch(g, b, again):
                rows = bass.ds(g * N, N)
                if again:
                    sp.wait_ge(zs, g - 1)
                    sp.wait_ge(x1s, g - 1)
                    sp.sem_inc(turns_pool, 1)
                sp.dma_start(h[:, b], K.h_dram[rows, :].rearrange("(j p) n -> p j n", p=TN)).then_inc(in_h[b], 16)
                sp.dma_start(xr[:, b], A.x[rows, :].rearrange("(j p) n -> p j n", p=TN)).then_inc(in_x[b], 16)

            def store(g, b):
                sp.wait_ge(results, NT * g + NT)
                sp.sem_inc(turns_pool, 1)
                sp.dma_start(out[bass.ds(g * N, N), :].rearrange("(j p) n -> p j n", p=TN), res[:, b])\
                  .then_inc(out_done[b], 16)

            fetch(0, 0, False)
            fetch(1, 1, False)

            def step(g, b, more, back):
                if more and not is_int(g, GR - 2):
                    fetch(g + 2, b, True)
                if back:
                    store(g - 1, 1 - b)
            groups(sp, step)
            sp.wait_ge(out_done[0], 16 * ((GR + 1) // 2))
            sp.wait_ge(out_done[1], 16 * (GR // 2))

        WEIGHTS = 16 * (6 + 5 * NE + 7 + 4)

        @block.gpsimd
        def _(pool):
            nc.gpsimd.memset(ones[:], 1.0).then_inc(consts, 1)
            nc.gpsimd.memset(minus_half[:], -0.5).then_inc(consts, 1)
            nc.gpsimd.memset(earlier[:], 1.0).then_inc(consts, 1)
            pool.wait_ge(consts, 3)
            nc.gpsimd.memset(a2[E2:E2 + 1], 1.0).then_inc(consts, 1)
            pool.wait_ge(consts, 4)
            nc.gpsimd.affine_select(out=earlier[:], in_=earlier[:], compare_op=ALU.is_gt, fill=0.0, base=0,
                                    pattern=[[1, NE], [-1, NE]], channel_multiplier=0).then_inc(consts, 1)

            def power(n):
                pool.wait_ge(vars_, n)
                pool.sem_inc(turns_pool, 1)
                nc.gpsimd.tensor_tensor(rstd[:], var[:], minus_half[0:TN, :], ALU.pow).then_inc(rstds, 1)

            power(1)

            def step(g, b, more, back):
                if not is_int(g, GR):
                    power(3 * g + 2)
                    power(3 * g + 3)
                if more:
                    power(3 * g + 4)
            groups(pool, step)

        @block.vector
        def _(dve):
            dve.wait_ge(consts, 5)
            nc.vector.tensor_single_scalar(K.denT[:], K.denT[:], 0.5, ALU.max).then_inc(rden, 1)
            dve.wait_ge(rden, 1)
            nc.vector.reciprocal(K.denT[:], K.denT[:]).then_inc(rden, 1)
            dve.wait_ge(weights, WEIGHTS)

            class Chain:
                def __init__(self, start):
                    self.at = start

                def then(self, ins):
                    self.at = self.at + 1
                    ins.then_inc(step_v, 1)
                    dve.wait_ge(step_v, self.at)

            def normalise(c, v, o, count, eps, gain):
                for j in range(NT):
                    last = nc.vector.bn_stats(stats[:, j, :], v[:, j, :])
                c.then(last)
                dve.sem_inc(turns, 1)
                for j in range(NT):
                    last = nc.vector.bn_aggr(mv[:, j, :], stats[:, j, :])
                c.then(last)
                nc.vector.tensor_single_scalar(var[:], mv[:, :, 1], eps, ALU.add).then_inc(vars_, 1)
                dve.wait_ge(rstds, count)
                for j in range(NT):
                    last = nc.vector.tensor_scalar(o[:, j, :], v[:, j, :], mv[:, j, 0:1], rstd[:, j:j + 1],
                                                   ALU.subtract, ALU.mult)
                if gain is None:
                    return last
                c.then(last)
                gb = [gains[0:TN, gain + i, :].unsqueeze(1).to_broadcast([TN, NT, D]) for i in range(2)]
                c.then(nc.vector.tensor_tensor(o, o, gb[0], ALU.mult))
                return nc.vector.tensor_tensor(o, o, gb[1], ALU.add)

            def spread_out(g):
                dve.wait_ge(spread, g + 1)
                if not is_int(g, 0):
                    dve.wait_ge(projected, g)
                nc.vector.tensor_tensor(attn[:], K.attT[:, :, bass.ds(g * N, N)], den_ps[:], ALU.mult)\
                    .then_inc(normed, 1)

            def first_norm(g, b, c):
                dve.wait_ge(projected, g + 1)
                dve.wait_ge(in_h[b], (g - b) * 8 + 16)
                nc.vector.tensor_tensor(z[:], ya_ps[:], h[:, b], ALU.add).then_inc(zs, 1)
                dve.wait_ge(zs, g + 1)
                normalise(c, z[:], pre[:, b], 3 * g + 1, 1e-12, 0).then_inc(pres, 1)

            def second_norm(g, b, c):
                dve.wait_ge(downs, g + 1)
                dve.wait_ge(pres, g + 1)
                c.then(nc.vector.tensor_tensor(z2[:], yb_ps[:], pre[:, b], ALU.add))
                dve.wait_ge(in_x[b], (g - b) * 8 + 16)
                c.then(normalise(c, z2[:], z2[:], 3 * g + 2, 1e-12, 2))
                nc.vector.tensor_tensor(x1[:, b], z2[:], xr[:, b], ALU.add).then_inc(x1s, 1)
                dve.wait_ge(x1s, g + 1)
                if not (is_int(g, 0) or is_int(g, 1)):
                    dve.wait_ge(preTs, 2 * g - 2)
                normalise(c, x1[:, b], xn[:, b], 3 * g + 3, 1e-5, None).then_inc(xns, 1)

            wide = g1[:].unsqueeze(2).to_broadcast([TN, NT, NE])

            def gates(g, c):
                dve.wait_ge(logits, g + 1)
                c.then(nc.vector.tensor_tensor(lg[:], yb_ps[:, :, 0:NE],
                                               g_b[0:TN, :].unsqueeze(1).to_broadcast([TN, NT, NE]), ALU.add))
                c.then(nc.vector.tensor_reduce(g1[:], lg[:], AX.X, ALU.max))
                nc.vector.tensor_tensor(g2[:], lg[:], wide, ALU.subtract).then_inc(ex_in, 1)
                dve.wait_ge(ex_out, 2 * g + 1)
                c.then(nc.vector.tensor_reduce(g1[:], g3[:], AX.X, ALU.add))
                c.then(nc.vector.reciprocal(g1[:], g1[:]))
                c.then(nc.vector.tensor_tensor(pg[:], g3[:], wide, ALU.mult))
                c.then(nc.vector.tensor_reduce(g1[:], pg[:], AX.X, ALU.max))
                nc.vector.tensor_tensor(g2[:], pg[:], wide, ALU.subtract).then_inc(ex_in, 1)
                mine = pg[:].unsqueeze(3).to_broadcast([TN, NT, NE, NE])
                other = pg[:].unsqueeze(2).to_broadcast([TN, NT, NE, NE])
                c.then(nc.vector.tensor_tensor(beats[:], other, mine, ALU.is_gt))
                c.then(nc.vector.tensor_tensor(ties[:], other, mine, ALU.is_equal))
                c.then(nc.vector.tensor_tensor(ties[:], ties[:],
                                               earlier[0:TN].unsqueeze(1).to_broadcast([TN, NT, NE, NE]), ALU.mult))
                c.then(nc.vector.tensor_tensor(beats[:], beats[:], ties[:], ALU.add))
                c.then(nc.vector.tensor_reduce(wt[:], beats[:], AX.X, ALU.add))
                c.then(nc.vector.tensor_single_scalar(wt[:], wt[:], 2.0, ALU.is_lt))

            def gate_weights(g, c):
                dve.wait_ge(ex_out, 2 * g + 2)
                c.then(nc.vector.tensor_tensor(wt[:], wt[:], g3[:], ALU.mult))
                c.then(nc.vector.tensor_reduce(g1[:], wt[:], AX.X, ALU.add))
                c.then(nc.vector.reciprocal(g1[:], g1[:]))
                nc.vector.tensor_tensor(wt[:], wt[:], wide, ALU.mult).then_inc(lgs, 1)

            def finish(g, b, c):
                dve.wait_ge(lgs, g + 1)
                if not (is_int(g, 0) or is_int(g, 1)):
                    dve.wait_ge(out_done[b], (g - b) * 8)
                for j in range(NT):
                    r = res[:, b, j, :]
                    for i in range(3):
                        dve.wait_ge(outs, 3 * NT * g + 3 * j + i + 1)
                        ps = o_ps[i % 2]
                        if i == 0:
                            c.then(nc.vector.tensor_tensor(r, ps[:, 0, :], x1[:, b, j, :], ALU.add))
                        for k, e in ((1, 0),) if i == 0 else ((0, 1), (1, 2)) if i == 1 else ((0, 3),):
                            last = nc.vector.scalar_tensor_tensor(
                                out=r, in0=ps[:, k, :], scalar=wt[:, j, e:e + 1], in1=r,
                                op0=ALU.mult, op1=ALU.add)
                            if (i, k) == (1, 0):
                                c.then(last)
                        last.then_inc(used if i < 2 else results, 1)
                        if i < 2:
                            dve.wait_ge(used, 2 * NT * g + 2 * j + i + 1)

            LA = 4
            LB = 1 + 5 + 2
            LC = 15 + 2 * NT

            spread_out(0)
            first_norm(0, 0, Chain(0))

            def step(g, b, more, back):
                base = LA + g * (LA + LB) + (0 if is_int(g, 0) else (g - 1) * LC)
                if is_int(g, GR):
                    base = LA * GR + LB * GR + (GR - 1) * LC
                if more:
                    spread_out(g + 1)
                c = Chain(base)
                if back:
                    gates(g - 1, c)
                if not is_int(g, GR):
                    second_norm(g, b, c)
                if more:
                    first_norm(g + 1, 1 - b, c)
                if back:
                    gate_weights(g - 1, c)
                    finish(g - 1, 1 - b, c)
                want = base + (0 if is_int(g, GR) else LB) + (LA if more else 0) + (LC if back else 0)
                if isinstance(g, int):
                    assert c.at == want, (g, c.at, want)
            groups(dve, step)

        @block.tensor
        def _(pe):
            pe.wait_ge(weights, WEIGHTS)
            pe.wait_ge(consts, 5)
            pe.wait_ge(rden, 2)

            def spread_sums(g):
                if not is_int(g, 0):
                    pe.wait_ge(normed, g)
                for k in range(2):
                    last = nc.tensor.matmul(den_ps[:, k, :], K.spreader[:, k * P:(k + 1) * P],
                                            K.denT[:, bass.ds(g * N, N)], start=True, stop=True)
                last.then_inc(spread, 1)

            def project(g):
                pe.wait_ge(normed, g + 1)
                if not is_int(g, 0):
                    pe.wait_ge(zs, g)
                for j in range(NT):
                    for k in range(2):
                        last = nc.tensor.matmul(ya_ps[:, j, :], attn[:, k, j * TN:(j + 1) * TN], w_o[:, k, :],
                                                start=k == 0, stop=k == 1)
                last.then_inc(projected, 1)

            def turn(rows, count):
                pe.sem_inc(turns_pe, 1)
                for j in range(NT):
                    for k in range(2):
                        last = nc.tensor.transpose(tr_ps[:, k, j * TN:(j + 1) * TN], rows[:, j, k * P:(k + 1) * P],
                                                   K.ident[0:TN, 0:TN])
                last.then_inc(preTs, 1)
                pe.wait_ge(copied, count)

            def mm_free(n, none=False):
                if not none:
                    pe.wait_ge(acts, n - 1)

            def gelu_layer(g, b):
                pe.wait_ge(pres, g + 1)
                turn(pre[:, b], 2 * g + 1)
                at = mm_base(g, False)
                for m in range(FM):
                    mm_free(at + m, is_int(g, 0) and m < 2)
                    for i in range(2):
                        for k in range(2):
                            c = 2 * m + i
                            last = nc.tensor.matmul(mm_ps[m % 2][:, i, :], w_i[:, k, c * P:(c + 1) * P],
                                                    preT[:, k, :], start=k == 0, stop=k == 1)
                    last.then_inc(mms, 1)
                if not is_int(g, 0):
                    pe.wait_ge(x1s, g)
                    pe.wait_ge(ex_in, 2 * g - 1)
                pe.wait_ge(acts, at + FM)
                for j in range(NT):
                    for c in range(FC):
                        last = nc.tensor.matmul(yb_ps[:, j, :], inter[:, c, j * TN:(j + 1) * TN], w_2[:, c, :],
                                                start=c == 0, stop=c == FC - 1)
                last.then_inc(downs, 1)

            def gate_logits(g, b):
                pe.wait_ge(xns, g + 1)
                turn(xn[:, b], 2 * g + 2)
                pe.wait_ge(x1s, g + 1)
                for j in range(NT):
                    for k in range(2):
                        last = nc.tensor.matmul(yb_ps[:, j, 0:NE], xnT[:, k, j * TN:(j + 1) * TN], g_w[:, k, :],
                                                start=k == 0, stop=k == 1)
                last.then_inc(logits, 1)

            def experts(g, b):
                at = mm_base(g, True)

                def pair(m, parts):
                    mm_free(at + m)
                    for i, p in enumerate(parts):
                        for k, (w, v) in enumerate(p):
                            last = nc.tensor.matmul(mm_ps[m % 2][0:w.shape[-1], i, :], w, v,
                                                    start=k == 0, stop=k == len(p) - 1)
                    last.then_inc(mms, 1)

                both = (0, 1)
                pair(0, [[(s_w1[:, k, i * P:(i + 1) * P], xnT[:, k, :]) for k in both] for i in both])
                pair(1, [[(e_w1[:, e, k, :], xnT[:, k, :]) for k in both] for e in (0, 1)])
                pair(2, [[(e_w1[:, e, k, :], xnT[:, k, :]) for k in both] for e in (2, 3)])
                pair(3, [[(s_w2[:, k, :], h1[:, k, :]) for k in both]])
                pe.wait_ge(acts, at + 2)
                pair(4, [[(e_w2[:, e, :], a1[:, e, :])] for e in (0, 1)])
                pe.wait_ge(acts, at + 3)
                pair(5, [[(e_w2[:, e, :], a1[:, e, :])] for e in (2, 3)])
                pe.wait_ge(acts, at + 6)
                if not is_int(g, 0):
                    pe.wait_ge(results, NT * g)
                for j in range(NT):
                    nodes = slice(j * TN, (j + 1) * TN)

                    def expert(o, e):
                        return nc.tensor.matmul(o, a2[:, e, nodes], e_w3[:, e, :], start=True, stop=True)

                    if j:
                        pe.wait_ge(results, NT * g + j)
                    nc.tensor.matmul(o_ps[0][:, 0, :], h2[:, nodes], s_w3[:], start=True, stop=False)
                    nc.tensor.matmul(o_ps[0][:, 0, :], ones[:, 0:TN], s_b3[:], start=False, stop=True)
                    expert(o_ps[0][:, 1, :], 0).then_inc(outs, 1)
                    expert(o_ps[1][:, 0, :], 1)
                    expert(o_ps[1][:, 1, :], 2).then_inc(outs, 1)
                    pe.wait_ge(used, 2 * NT * g + 2 * j + 1)
                    expert(o_ps[0][:, 0, :], 3).then_inc(outs, 1)

            spread_sums(0)
            project(0)

            def step(g, b, more, back):
                if more:
                    spread_sums(g + 1)
                if back:
                    gate_logits(g - 1, 1 - b)
                if not is_int(g, GR):
                    gelu_layer(g, b)
                if more:
                    project(g + 1)
                if back:
                    experts(g - 1, 1 - b)
            groups(pe, step)

        @block.scalar
        def _(act):
            act.wait_ge(weights, WEIGHTS)
            act.wait_ge(consts, 5)

            def step(g, b, more, back):
                p = g - 1
                if back:
                    act.wait_ge(preTs, 2 * p + 2)
                    nc.scalar.activation(xnT[:], tr_ps[:], ACT.Copy).then_inc(copied, 1)
                if not is_int(g, GR):
                    act.wait_ge(preTs, 2 * g + 1)
                    nc.scalar.activation(preT[:], tr_ps[:], ACT.Copy).then_inc(copied, 1)
                if back:
                    act.wait_ge(ex_in, 2 * p + 1)
                    nc.scalar.activation(g3[:], g2[:], ACT.Exp).then_inc(ex_out, 1)
                if not is_int(g, GR):
                    at = mm_base(g, False)
                    for m in range(FM):
                        act.wait_ge(mms, at + m + 1)
                        if m == 0 and not is_int(g, 0):
                            act.wait_ge(downs, g)
                        nc.scalar.activation(inter[:, 2 * m:2 * m + 2, :], mm_ps[m % 2][:], ACT.Gelu)\
                            .then_inc(acts, 1)
                if back:
                    at = mm_base(p, True)
                    act.wait_ge(ex_in, 2 * p + 2)
                    nc.scalar.activation(g3[:], g2[:], ACT.Exp).then_inc(ex_out, 1)
                    act.wait_ge(mms, at + 1)
                    for i in range(2):
                        last = nc.scalar.activation(h1[:, i, :], mm_ps[0][:, i, :], ACT.Relu, bias=s_b1[:, i:i + 1])
                    last.then_inc(acts, 1)
                    for m in (1, 2):
                        act.wait_ge(mms, at + m + 1)
                        for i in range(2):
                            e = 2 * (m - 1) + i
                            last = nc.scalar.activation(a1[:, e, :], mm_ps[m % 2][:, i, :], ACT.Relu,
                                                        bias=e_b1[:, e:e + 1])
                        last.then_inc(acts, 1)
                    act.wait_ge(mms, at + 4)
                    nc.scalar.activation(h2[:], mm_ps[1][:, 0, :], ACT.Relu, bias=s_b2[:]).then_inc(acts, 1)
                    for m in (4, 5):
                        act.wait_ge(mms, at + m + 1)
                        for i in range(2):
                            e = 2 * (m - 4) + i
                            last = nc.scalar.activation(a2[0:E2, e, :], mm_ps[m % 2][0:E2, i, :], ACT.Relu,
                                                        bias=e_b2[:, e:e + 1])
                        last.then_inc(acts, 1)
            groups(act, step)


class Kept:
    pass


def bass_gnn_ffn(nc, x, src, dst, w_qkv, w_o, ln1_g, ln1_b, w_i, w_out2, ln2_g, ln2_b, s_w1, s_b1, s_w2, s_b2,
                 s_w3, s_b3, e_w1, e_b1, e_w2, e_b2, e_w3, e_b3, g_w, g_b, out):
    S = Shape(x.shape[0], src.shape[0], x.shape[1], 8)
    K = Kept()
    A = Kept()
    A.x, A.w_o, A.ln1_g, A.ln1_b, A.w_i, A.w_out2, A.ln2_g, A.ln2_b = x, w_o, ln1_g, ln1_b, w_i, w_out2, ln2_g, ln2_b
    A.s_w1, A.s_b1, A.s_w2, A.s_b2, A.s_w3, A.s_b3 = s_w1, s_b1, s_w2, s_b2, s_w3, s_b3
    A.e_w1, A.e_b1, A.e_w2, A.e_b2, A.e_w3, A.e_b3, A.g_w, A.g_b = e_w1, e_b1, e_w2, e_b2, e_w3, e_b3, g_w, g_b
    K.h_dram = nc.dram_tensor("h_rows", [S.V, S.D], F32).ap()
    K.q_dram = nc.dram_tensor("q_rows", [S.V, S.D], F32).ap()
    K.kv_dram = nc.dram_tensor("kv_rows", [S.V, 2 * S.D], F32).ap()
    K.slot_table = nc.dram_tensor("slot_table", [S.SLOTS, 1], I32).ap()
    K.mark_table = nc.dram_tensor("mark_table", [S.ROWS, 1], F32).ap()
    K.flag_table = nc.dram_tensor("flag_table", [S.ROWS + 1], F32).ap()
    K.node_table = nc.dram_tensor("node_table", [S.ROWS], I32).ap()
    with ExitStack() as ctx:
        K.stack = ctx
        def sb(name, shape, dt, into=ctx):
            return into.enter_context(nc.sbuf_tensor(name, shape, dt))

        K.ident = sb("ident", [S.P, S.P], F32)
        K.ident_b = sb("ident_b", [S.P, S.P], BF16)
        K.before = sb("before", [S.P, S.P], F32)
        K.before_b = sb("before_b", [S.P, S.P], BF16)
        K.iota_i = sb("iota_i", [S.P, S.P], I32)
        K.iota_b = sb("iota_b", [S.P, S.P], BF16)
        K.iota_f = sb("iota_f", [S.P, S.P], F32)
        K.is_node = sb("is_node", [S.BLK, S.P], F32)
        with ExitStack() as edges:
            K.dst_i = sb("dst_i", [S.P, S.EC], I32, edges)
            K.hi = sb("hi", [S.P, S.EC + S.G], BF16, edges)
            K.lo = sb("lo", [S.P, S.EC + S.G], BF16, edges)
            K.pad = sb("pad", [S.P, S.EC], BF16, edges)
            K.degree = sb("degree", [S.BLK, S.P], F32, edges)
            K.pointer = sb("pointer", [S.BLK, 2, S.G + 1, S.P], F32, edges)
            build_prepare(nc, S, K, x, src, dst, w_qkv)
            build_rows(nc, S, K)
            build_slots(nc, S, K)
        K.attT = sb("attT", [S.P, 2, S.V + S.P], F32)
        K.denT = sb("denT", [S.H, S.V + S.P], F32)
        K.spreader = sb("spreader", [S.H, S.D], F32)
        build_attention(nc, S, K)
        build_dense(nc, S, K, A, out)


_INS = ["x", "src", "dst", "L0_gnn_W_qkv", "L0_gnn_W_o", "L0_gnn_ln1_g", "L0_gnn_ln1_b", "L0_gnn_W_i",
        "L0_gnn_W_out2", "L0_gnn_ln2_g", "L0_gnn_ln2_b", "L0_ffn_sW1", "L0_ffn_sb1", "L0_ffn_sW2", "L0_ffn_sb2",
        "L0_ffn_sW3", "L0_ffn_sb3", "L0_ffn_eW1", "L0_ffn_eb1", "L0_ffn_eW2", "L0_ffn_eb2", "L0_ffn_eW3",
        "L0_ffn_eb3", "L0_ffn_gW", "L0_ffn_gb"]


def kernel(**inputs):
    import numpy as _np
    import concourse.bacc as _bacc
    from concourse import mybir as _mybir
    from concourse.bass_utils import run_bass_kernel_spmd as _run

    nc = _bacc.Bacc("TRN2", target_bir_lowering=False, num_devices=1)
    arrays, args = {}, []
    for name in _INS:
        a = _np.ascontiguousarray(inputs[name])
        arrays[f"in_{name}_dram"] = a
        args.append(nc.dram_tensor(f"in_{name}_dram", a.shape, _mybir.dt.from_np(a.dtype), kind="ExternalInput").ap())
    x = inputs["x"]
    out = nc.dram_tensor("out_0_dram", x.shape, _mybir.dt.from_np(_np.dtype("float32")), kind="ExternalOutput").ap()
    bass_gnn_ffn(nc, *args, out)
    r = _run(nc, [arrays], core_ids=[0])
    return r.results[0]["out_0_dram"]
```

```python
import concourse.bass as bass
from concourse import mybir
from contextlib import ExitStack

F32, BF16, I32 = mybir.dt.float32, mybir.dt.bfloat16, mybir.dt.int32
ALU, ACT, AX = mybir.AluOpType, mybir.ActivationFunctionType, mybir.AxisListType


class Shape:

    def __init__(s, nodes, edges, dim, heads):
        s.P = 128
        s.V, s.E, s.D, s.H = nodes, edges, dim, heads
        s.HD = dim // heads
        s.BLK = -(-nodes // s.P)
        s.TAIL = nodes - (s.BLK - 1) * s.P
        s.G = 8
        s.EC = -(-edges // s.P)
        s.EC = -(-s.EC // (4 * s.G)) * 4 * s.G
        s.GROUPS = s.EC // s.G
        s.SL = 8
        s.NB = 4
        s.MB = 8
        rows = -(-(edges + s.SL * nodes) // s.SL)
        s.RT = -(-rows // s.P)
        s.RT = -(-s.RT // s.MB) * s.MB
        s.ROWS = s.RT * s.P
        s.SLOTS = s.ROWS * s.SL
        s.NT = 2
        s.TN = max(n for n in range(1, s.P + 1) if nodes % (s.NT * n) == 0)
        s.NOWHERE = 1.0e6
        s.NEG = -1.0e30
        s.EMPTY = -1.0e20


def build_prepare(nc, S, K, x, src, dst, w_qkv):
    P, D = S.P, S.D
    with ExitStack() as ctx:
        def sb(name, shape, dt):
            return ctx.enter_context(nc.sbuf_tensor(f"prep_{name}", shape, dt))

        def pb(name, shape, dt):
            return ctx.enter_context(nc.psum_tensor(f"prep_{name}", shape, dt))

        def sem(name):
            return K.stack.enter_context(nc.semaphore(f"prep_{name}"))

        src_i = sb("src_i", [P, S.EC], I32)
        part_i = sb("part_i", [P, S.EC], I32)
        w_sb = sb("w_qkv", [P, 2, 3 * D], F32)
        xt = sb("xt", [P, 2, D], F32)
        stats = sb("stats", [P, 2, 6], F32)
        mv = sb("mv", [P, 2, 2], F32)
        std = sb("std", [P, 2, 1], F32)
        rstd = sb("rstd", [P, 2, 1], F32)
        eps = sb("eps", [P, 1], F32)
        ht = sb("ht", [P, 2, D], F32)
        hT = sb("hT", [P, 2, 2, P], F32)
        qkv = sb("qkv", [P, 2, 3 * D], F32)
        GPT = S.GROUPS // S.BLK
        hi1 = sb("hi1", [P, GPT, S.BLK, S.G], BF16)
        lo1 = sb("lo1", [P, GPT, P, S.G], BF16)
        iota_wide = sb("iota_wide", [P, P, S.G], BF16)
        empty_slots = sb("empty_slots", [P, S.SLOTS // P], I32)
        zero_marks = sb("zero_marks", [P, S.RT], F32)

        hT_ps = pb("hT_ps", [P, 2, P], F32)
        kv_ps = pb("kv_ps", [P, 2 * D], F32)
        q_ps = pb("q_ps", [P, D], F32)
        deg_ps = pb("deg_ps", [P, S.BLK], F32)

        src_in, dst_in, w_in = sem("src_in"), sem("dst_in"), sem("w_in")
        x_in = [sem("x_in0"), sem("x_in1")]
        const, filled, tables = sem("const"), sem("filled"), sem("tables")
        lohi = sem("lohi")
        bn, mvd, sq, rs, hn = sem("bn"), sem("mvd"), sem("sq"), sem("rs"), sem("hn")
        tr, hTd, mm, kvd, qd = sem("tr"), sem("hTd"), sem("mm"), sem("kvd"), sem("qd")
        stored = [sem("stored0"), sem("stored1")]
        ones_ok, counted = sem("ones_ok"), sem("counted")
        degrees = sem("degrees")
        turns, turns_sp = sem("turns"), sem("turns_sp")

        block = ctx.enter_context(nc.Block())
        assert GPT * S.BLK == S.GROUPS and GPT % 2 == 0 and S.BLK % 2 == 1

        def tiles(engine, step):
            step(0, 0, P, True)
            step(1, 1, P, True)
            step(2, 0, P, False)
            step(3, 1, P, False)
            with engine.Fori(2, S.BLK // 2) as i:
                step(2 * i, 0, P, False)
                step(2 * i + 1, 1, P, False)
            step(S.BLK - 1, 0, S.TAIL, False)

        @block.sync
        def _(sp):
            full = S.E // S.EC
            rest = S.E - full * S.EC
            cut = full // 16 * 16
            rows = S.E // S.EC * S.EC
            sp.wait_ge(filled, 2)
            for table, edges, done in ((src_i, src, src_in), (K.dst_i, dst, dst_in)):
                v = edges[0:rows].rearrange("(p c) -> p c", c=S.EC)
                sp.dma_start(table[0:cut, :], v[0:cut, :]).then_inc(done, 16)
                sp.dma_start(table[cut:full, :], v[cut:full, :]).then_inc(done, 16)
                sp.dma_start(table[full:full + 1, 0:rest],
                             edges[rows:S.E].rearrange("(a c) -> a c", a=1)).then_inc(done, 16)
            sp.dma_start(w_sb[:], w_qkv.rearrange("(k p) n -> p k n", p=P)).then_inc(w_in, 16)
            sp.wait_ge(filled, 4)
            sp.dma_start(K.slot_table.rearrange("(p c) o -> p (c o)", p=P), empty_slots[:]).then_inc(tables, 16)
            sp.dma_start(K.mark_table.rearrange("(p c) o -> p (c o)", p=P), zero_marks[:]).then_inc(tables, 16)

            def step(t, b, n, first):
                if not first:
                    sp.wait_ge(hn, t - 1)
                    sp.sem_inc(turns_sp, 1)
                sp.dma_start(xt[0:n, b, :], x[bass.ds(t * P, n), :]).then_inc(x_in[b], 16)
            tiles(sp, step)
            sp.wait_ge(dst_in, 48)
            sp.wait_ge(tables, 32)

        @block.gpsimd
        def _(pool):
            nc.gpsimd.memset(src_i[:], 64 * P - 1).then_inc(filled, 1)
            nc.gpsimd.memset(K.dst_i[:], 0).then_inc(filled, 1)
            nc.gpsimd.memset(empty_slots[:], S.V).then_inc(filled, 1)
            nc.gpsimd.memset(zero_marks[:], 0.0).then_inc(filled, 1)
            nc.gpsimd.iota(K.iota_i[:], pattern=[[1, P]], base=0, channel_multiplier=0).then_inc(const, 1)
            nc.gpsimd.memset(K.ident[:], 0.0).then_inc(const, 1)
            nc.gpsimd.memset(K.before[:], 1.0).then_inc(const, 1)
            nc.gpsimd.memset(K.is_node[:], 1.0).then_inc(const, 1)
            nc.gpsimd.memset(eps[:], 1e-5).then_inc(const, 1)
            pool.wait_ge(const, 5)
            nc.gpsimd.affine_select(out=K.ident[:], in_=K.ident[:], compare_op=ALU.not_equal, fill=1.0, base=0,
                                    pattern=[[-1, P]], channel_multiplier=1).then_inc(const, 1)
            nc.gpsimd.affine_select(out=K.before[:], in_=K.before[:], compare_op=ALU.is_gt, fill=0.0, base=0,
                                    pattern=[[1, P]], channel_multiplier=-1).then_inc(const, 1)
            nc.gpsimd.affine_select(out=K.is_node[:], in_=K.is_node[:], compare_op=ALU.is_gt, fill=0.0, base=S.V,
                                    pattern=[[-P, S.BLK]], channel_multiplier=-1).then_inc(const, 1)
            pool.wait_ge(const, 8)
            nc.gpsimd.tensor_copy(K.ident_b[:], K.ident[:]).then_inc(const, 1)
            nc.gpsimd.tensor_copy(K.before_b[:], K.before[:]).then_inc(const, 1)
            nc.gpsimd.tensor_copy(K.iota_b[:], K.iota_i[:]).then_inc(const, 1)
            nc.gpsimd.tensor_copy(K.iota_f[:], K.iota_i[:]).then_inc(const, 1)
            nc.gpsimd.tensor_copy(iota_wide[:], K.iota_i[:].unsqueeze(2).to_broadcast([P, P, S.G])).then_inc(const, 1)

        @block.vector
        def _(dve):
            dve.wait_ge(src_in, 48)
            nc.vector.tensor_single_scalar(part_i[:], src_i[:], P - 1, ALU.bitwise_and).then_inc(lohi, 1)
            dve.wait_ge(lohi, 1)
            nc.vector.tensor_copy(K.lo[:, 0:S.EC], part_i[:]).then_inc(lohi, 1)
            dve.wait_ge(lohi, 2)
            nc.vector.tensor_single_scalar(part_i[:], src_i[:], 7, ALU.arith_shift_right).then_inc(lohi, 1)
            dve.wait_ge(lohi, 3)
            nc.vector.tensor_copy(K.hi[:, 0:S.EC], part_i[:]).then_inc(lohi, 1)
            nc.vector.tensor_scalar(K.pad[:], src_i[:], float(S.V), S.NOWHERE, ALU.is_ge, ALU.mult).then_inc(lohi, 1)
            nc.vector.memset(K.lo[:, S.EC:], 0).then_inc(lohi, 1)
            nc.vector.memset(K.hi[:, S.EC:], 0).then_inc(lohi, 1)
            dve.wait_ge(lohi, 7)
            dve.wait_ge(const, 13)

            def step(t, b, n, first):
                dve.wait_ge(x_in[b], (t - b) * 8 + 16)
                nc.vector.bn_stats(stats[0:n, b, :], xt[0:n, b, :]).then_inc(bn, 1)
                dve.wait_ge(bn, t + 1)
                dve.sem_inc(turns, 1)
                nc.vector.bn_aggr(mv[0:n, b, :], stats[0:n, b, :]).then_inc(mvd, 1)
                for j in range(GPT):
                    g = GPT * t + j
                    if not (first and b == 0):
                        dve.wait_ge(counted, g - GPT + 1)
                    for one_hot, part, size in ((hi1, K.hi, S.BLK), (lo1, K.lo, P)):
                        last = nc.vector.tensor_tensor(
                            one_hot[:, j], iota_wide[:, 0:size, :],
                            part[:, bass.ds(g * S.G, S.G)].unsqueeze(1).to_broadcast([P, size, S.G]), ALU.is_equal)
                    last.then_inc(ones_ok, 1)
                    if j == 1:
                        dve.wait_ge(sq, t + 1)
                        nc.vector.reciprocal(rstd[0:n, b, :], std[0:n, b, :]).then_inc(rs, 1)
                        dve.wait_ge(rs, t + 1)
                        if not first:
                            dve.wait_ge(stored[b], (t - b) * 24)
                            dve.wait_ge(tr, t - 1)
                        nc.vector.tensor_scalar(ht[0:n, b, :], xt[0:n, b, :], mv[0:n, b, 0:1], rstd[0:n, b, :],
                                                ALU.subtract, ALU.mult).then_inc(hn, 1)
                    if j == 2 and not (first and b == 0):
                        take_kv(t - 1, 1 - b, P, first or (isinstance(t, int) and t == 2))

            def take_kv(t, b, n, first):
                dve.wait_ge(mm, t + 1)
                if not first:
                    dve.wait_ge(stored[b], (t - b) * 24)
                nc.vector.tensor_copy(qkv[0:n, b, D:3 * D], kv_ps[0:n, :]).then_inc(kvd, 1)

            tiles(dve, step)
            take_kv(S.BLK - 1, 0, S.TAIL, False)
            dve.wait_ge(counted, S.GROUPS)
            nc.vector.tensor_copy(K.degree[:], deg_ps[:]).then_inc(degrees, 1)

        @block.scalar
        def _(act):
            act.wait_ge(const, 13)

            def take_q(t, b, n, first):
                act.wait_ge(mm, t + 1)
                if not first:
                    act.wait_ge(stored[b], (t - b) * 24)
                nc.scalar.activation(qkv[0:n, b, 0:D], q_ps[0:n, :], ACT.Copy,
                                     scale=float(S.HD) ** -0.5).then_inc(qd, 1)
                rows = bass.ds(t * P, n)
                act.dma_start(K.h_dram[rows, :], ht[0:n, b, :]).then_inc(stored[b], 16)
                act.wait_ge(qd, t + 1)
                act.dma_start(K.q_dram[rows, :], qkv[0:n, b, 0:D]).then_inc(stored[b], 16)

            def store_kv(t, b, n):
                act.wait_ge(kvd, t + 1)
                act.dma_start(K.kv_dram[bass.ds(t * P, n), :], qkv[0:n, b, D:3 * D]).then_inc(stored[b], 16)

            def step(t, b, n, first):
                act.wait_ge(mvd, t + 1)
                nc.scalar.activation(std[0:n, b, :], mv[0:n, b, 1:2], ACT.Sqrt, bias=eps[0:n, :]).then_inc(sq, 1)
                one_before = not (first and b == 0)
                if one_before:
                    take_q(t - 1, 1 - b, P, first or (isinstance(t, int) and t == 2))
                act.wait_ge(tr, t + 1)
                nc.scalar.activation(hT[:, b, :, 0:n], hT_ps[:, :, 0:n], ACT.Copy).then_inc(hTd, 1)
                if one_before:
                    store_kv(t - 1, 1 - b, P)
            tiles(act, step)
            take_q(S.BLK - 1, 0, S.TAIL, False)
            store_kv(S.BLK - 1, 0, S.TAIL)
            act.wait_ge(stored[0], 48 * ((S.BLK + 1) // 2))
            act.wait_ge(stored[1], 48 * (S.BLK // 2))

        @block.tensor
        def _(pe):
            pe.wait_ge(w_in, 16)
            pe.wait_ge(const, 13)
            wv = w_sb[:].rearrange("p k (h c i) -> p k c h i", c=3, i=S.HD)

            def step(t, b, n, first):
                for j in range(GPT):
                    g = GPT * t + j
                    pe.wait_ge(ones_ok, g + 1)
                    last_group = not first and isinstance(t, int) and j == GPT - 1
                    for c in range(S.G):
                        last = nc.tensor.matmul(deg_ps[:], lo1[:, j, :, c], hi1[:, j, :, c],
                                                start=(first and b == 0 and j == 0 and c == 0),
                                                stop=(last_group and c == S.G - 1), skip_group_check=True)
                    last.then_inc(counted, 1)
                    if j == 2:
                        pe.wait_ge(hn, t + 1)
                        if not (first and b == 0):
                            pe.wait_ge(hTd, t)
                        for k in range(2):
                            last = nc.tensor.transpose(hT_ps[:, k, 0:n], ht[0:n, b, k * P:(k + 1) * P],
                                                       K.ident[0:n, 0:n])
                        last.then_inc(tr, 1)
                pe.wait_ge(hTd, t + 1)
                if not (first and b == 0):
                    pe.wait_ge(kvd, t)
                    pe.wait_ge(qd, t)
                for k in range(2):
                    nc.tensor.matmul(q_ps[0:n, :], hT[:, b, k, 0:n], wv[:, k, 0], start=k == 0, stop=k == 1)
                for c in range(2):
                    for k in range(2):
                        last = nc.tensor.matmul(kv_ps[0:n, c * D:(c + 1) * D], hT[:, b, k, 0:n], wv[:, k, 1 + c],
                                                start=k == 0, stop=k == 1)
                last.then_inc(mm, 1)
            tiles(pe, step)


def build_rows(nc, S, K):
    P = S.P
    with ExitStack() as ctx:
        def sb(name, shape, dt):
            return ctx.enter_context(nc.sbuf_tensor(f"rows_{name}", shape, dt))

        def pb(name, shape, dt):
            return ctx.enter_context(nc.psum_tensor(f"rows_{name}", shape, dt))

        def sem(name):
            return K.stack.enter_context(nc.semaphore(f"rows_{name}"))

        di = sb("di", [P, S.BLK], I32)
        rows = sb("rows", [P, S.BLK], F32)
        ones = sb("ones", [P, S.RT], F32)
        total = sb("total", [P, S.BLK], F32)
        upto = sb("upto", [P, S.BLK], F32)
        base = sb("base", [P, 1], F32)
        start = sb("start", [P, S.BLK], F32)
        target = sb("target", [P, S.BLK], F32)
        target_i = sb("target_i", [P, S.BLK], I32)
        mark = sb("mark", [P, S.RT], F32)
        cum = sb("cum", [P, S.RT], F32)
        node = sb("node", [P, S.RT], I32)
        flag = sb("flag", [P, S.RT], F32)
        total_ps = pb("total_ps", [P, S.BLK], F32)
        below_ps = pb("below_ps", [P, S.BLK], F32)
        base_ps = pb("base_ps", [P, 1], F32)
        d, pm, ld, st, sc = sem("d"), sem("pm"), sem("ld"), sem("st"), sem("sc")
        row_counts, targets, cums, flags, nodes = (sem(n) for n in ("row_counts", "targets", "cums", "flags", "nodes"))
        block = ctx.enter_context(nc.Block())

        @block.vector
        def _(dve):
            n = [0]

            def then(ins):
                n[0] += 1
                ins.then_inc(d, 1)
                dve.wait_ge(d, n[0])

            then(nc.vector.memset(ones[:], 1.0))
            then(nc.vector.tensor_single_scalar(di[:], K.degree[:], float(S.SL - 1), ALU.add))
            then(nc.vector.tensor_single_scalar(di[:], di[:], 3, ALU.arith_shift_right))
            then(nc.vector.tensor_single_scalar(rows[:], di[:], 1.0, ALU.max))
            then(nc.vector.tensor_tensor(rows[:], rows[:], K.is_node[:], ALU.mult))
            dve.sem_inc(row_counts, 1)
            dve.wait_ge(pm, 1)
            then(nc.vector.tensor_copy(total[:], total_ps[:]))
            then(nc.vector.tensor_tensor_scan(upto[:], ones[:, 0:S.BLK], total[:], 0.0, ALU.mult, ALU.add))
            then(nc.vector.tensor_tensor(start[:], upto[:], total[:], ALU.subtract))
            then(nc.vector.tensor_tensor(start[:], below_ps[:], start[:], ALU.add))
            then(nc.vector.tensor_single_scalar(K.pointer[:, 1, S.G, :], start[:], float(S.SL), ALU.mult))
            then(nc.vector.tensor_scalar(target[:], K.is_node[:], -S.NOWHERE, S.NOWHERE, ALU.mult, ALU.add))
            nc.vector.tensor_tensor(target_i[:], target[:], start[:], ALU.add).then_inc(targets, 1)
            dve.wait_ge(ld, 16)
            nc.vector.tensor_tensor_scan(cum[:], ones[:], mark[:], 0.0, ALU.mult, ALU.add).then_inc(cums, 1)
            nc.vector.tensor_single_scalar(flag[:], mark[:], S.NEG, ALU.mult).then_inc(flags, 1)
            dve.wait_ge(pm, 2)
            then(nc.vector.tensor_copy(base[:], base_ps[:]))
            nc.vector.tensor_scalar(node[:], cum[:], base[:], -1.0, ALU.add, ALU.add).then_inc(nodes, 1)

        @block.tensor
        def _(pe):
            pe.wait_ge(row_counts, 1)
            nc.tensor.matmul(total_ps[:], ones[:, 0:P], rows[:], start=True, stop=True)
            nc.tensor.matmul(below_ps[:], K.before[:], rows[:], start=True, stop=True).then_inc(pm, 1)
            pe.wait_ge(cums, 1)
            nc.tensor.matmul(base_ps[:], K.before[:], cum[:, S.RT - 1:S.RT], start=True, stop=True).then_inc(pm, 1)

        @block.gpsimd
        def _(pool):
            pool.wait_ge(targets, 1)
            for c in range(S.BLK):
                pool.indirect_dma_start(
                    out=K.mark_table, out_offset=bass.IndirectOffsetOnAxis(ap=target_i[:, c:c + 1], axis=0),
                    in_=ones[:, 0:1], in_offset=None, bounds_check=S.ROWS - 1, oob_is_err=False).then_inc(sc, 16)
            pool.wait_ge(sc, 16 * S.BLK)

        @block.sync
        def _(sp):
            sp.wait_ge(sc, 16 * S.BLK)
            sp.dma_start(mark[:], K.mark_table.rearrange("(p c) o -> p (c o)", p=P)).then_inc(ld, 16)
            sp.wait_ge(flags, 1)
            sp.dma_start(K.flag_table[0:S.ROWS].rearrange("(p c) -> p c", p=P), flag[:]).then_inc(st, 16)
            sp.dma_start(K.flag_table[S.ROWS:S.ROWS + 1].rearrange("(p c) -> p c", p=1),
                         flag[0:1, 0:1]).then_inc(st, 16)
            sp.wait_ge(nodes, 1)
            sp.dma_start(K.node_table.rearrange("(p c) -> p c", p=P), node[:]).then_inc(st, 16)
            sp.wait_ge(st, 48)


def build_slots(nc, S, K):
    P, G, HALF = S.P, S.G, S.G // 2
    with ExitStack() as ctx:
        def sb(name, shape, dt):
            return ctx.enter_context(nc.sbuf_tensor(f"slots_{name}", shape, dt))

        def pb(name, shape, dt):
            return ctx.enter_context(nc.psum_tensor(f"slots_{name}", shape, dt))

        def sem(name):
            return K.stack.enter_context(nc.semaphore(f"slots_{name}"))

        hi1 = sb("hi1", [P, 2, G, S.BLK], BF16)
        lo1 = sb("lo1", [P, 2, G, P], BF16)
        loT_b = sb("loT_b", [P, G, P], BF16)
        loT_f = sb("loT_f", [P, G, P], F32)
        same = sb("same", [P, G, P], BF16)
        picked = sb("picked", [P, G, S.BLK], F32)
        slot_f = sb("slot_f", [P, 2, G], F32)
        slot_i = sb("slot_i", [P, 2, G], I32)
        dst_s = sb("dst_s", [P, 2, G], I32)
        loT_ps = [pb(f"loT_ps{h}", [P, HALF, P], BF16) for h in range(2)]
        same_ps = [pb(f"same_ps{h}", [P, HALF, P], F32) for h in range(2)]
        run_ps = [pb(f"run_ps{h}", [P, HALF, S.BLK], F32) for h in range(2)]
        at_ps = [pb(f"at_ps{h}", [P, HALF, S.BLK], F32) for h in range(2)]

        onehots = sem("onehots")
        turned = sem("turned")
        loT_ok = sem("loT_ok")
        grams = sem("grams")
        runs = sem("runs")
        masked = sem("masked")
        moved = sem("moved")
        looked = sem("looked")
        picks = sem("picks")
        slots = sem("slots")
        dsts = sem("dsts")
        scattered = [sem("scattered0"), sem("scattered1")]
        turns, turns_pe = sem("turns"), sem("turns_pe")
        block = ctx.enter_context(nc.Block())

        def groups(engine, step):
            step(0, 0, True)
            step(1, 1, True)
            with engine.Fori(1, S.GROUPS // 2) as i:
                step(2 * i, 0, False)
                step(2 * i + 1, 1, False)

        @block.vector
        def _(dve):
            def one_hots(g, b, first, col):
                if not first:
                    dve.wait_ge(looked, 2 * g - 2)
                nc.vector.tensor_tensor(
                    hi1[:, b], K.iota_b[:, 0:S.BLK].unsqueeze(1).to_broadcast([P, G, S.BLK]),
                    K.hi[:, col].unsqueeze(2).to_broadcast([P, G, S.BLK]), ALU.is_equal).then_inc(onehots, 1)
                nc.vector.tensor_tensor(
                    lo1[:, b], K.iota_b[:].unsqueeze(1).to_broadcast([P, G, P]),
                    K.lo[:, col].unsqueeze(2).to_broadcast([P, G, P]), ALU.is_equal).then_inc(onehots, 1)

            one_hots(0, 0, True, slice(0, G))

            def step(g, b, first):
                for h in range(2):
                    dve.wait_ge(runs, 2 * g + h + 1)
                    if not (first and b == 0 and h == 0):
                        dve.wait_ge(moved, 2 * g + h)
                    if not first or (b and h):
                        dve.wait_ge(looked, 2 * g - 2 + h)
                    before = K.pointer[:, b, HALF, :] if h else K.pointer[:, 1 - b, G, :]
                    nc.vector.tensor_tensor(K.pointer[:, b, 1 + h * HALF:1 + (h + 1) * HALF, :], run_ps[h][:],
                                            before.unsqueeze(1).to_broadcast([P, HALF, S.BLK]),
                                            ALU.add).then_inc(moved, 1)
                for h in range(2):
                    dve.wait_ge(grams, 2 * g + h + 1)
                    if not (first and b == 0):
                        dve.wait_ge(looked, 2 * g - 1 + h)
                    nc.vector.tensor_tensor(same[:, h * HALF:(h + 1) * HALF, :], same_ps[h][:],
                                            K.before_b[:].unsqueeze(1).to_broadcast([P, HALF, P]),
                                            ALU.mult).then_inc(masked, 1)
                one_hots(g + 1, 1 - b, first and b == 0, bass.ds((g + 1) * G, G))
                for c in range(G):
                    dve.wait_ge(looked, 2 * g + 1 + c // HALF)
                    if not first and c == 0:
                        dve.wait_ge(slots, g - 1)
                    nc.vector.tensor_tensor_reduce(out=picked[:, c, :], in0=at_ps[c // HALF][:, c % HALF, :],
                                                   in1=hi1[:, b, c, :], scale=1.0, scalar=0.0, op0=ALU.mult,
                                                   op1=ALU.add, accum_out=slot_f[:, b, c:c + 1]).then_inc(picks, 1)
                dve.wait_ge(picks, G * g + G)
                if not first:
                    dve.wait_ge(scattered[b], (g - b) * 8 * G)
                nc.vector.tensor_tensor(slot_i[:, b, :], slot_f[:, b, :], K.pad[:, bass.ds(g * G, G)],
                                        ALU.add).then_inc(slots, 1)
            groups(dve, step)

        @block.tensor
        def _(pe):
            def ahead(g, b, first):
                pe.wait_ge(onehots, 2 * g + 2)
                for h in range(2):
                    if not first:
                        pe.wait_ge(loT_ok, 4 * g - 2 + 2 * h)
                    pe.sem_inc(turns_pe, 1)
                    for c in range(HALF):
                        last = nc.tensor.transpose(loT_ps[h][:, c, :], lo1[:, b, h * HALF + c, :], K.ident_b[:])
                    last.then_inc(turned, 1)
                for h in range(2):
                    if not first:
                        pe.wait_ge(moved, 2 * g - 1 + h)
                    for c in range(HALF):
                        for k in range(c + 1):
                            last = nc.tensor.matmul(run_ps[h][:, c, :], lo1[:, b, h * HALF + k, :],
                                                    hi1[:, b, h * HALF + k, :], start=k == 0, stop=k == c)
                    last.then_inc(runs, 1)
                for h in range(2):
                    pe.wait_ge(loT_ok, 4 * g + 2 + 2 * h)
                    if not first:
                        pe.wait_ge(masked, 2 * g - 1 + h)
                    for c in range(HALF):
                        v = loT_b[:, h * HALF + c, :]
                        last = nc.tensor.matmul(same_ps[h][:, c, :], v, v, start=True, stop=True)
                    last.then_inc(grams, 1)

            def look(g, b, first):
                for h in range(2):
                    pe.wait_ge(moved, 2 * g + h + 1)
                    pe.wait_ge(masked, 2 * g + h + 1)
                    if not (first and b == 0):
                        pe.wait_ge(picks, G * g - HALF + h * HALF)
                    for c in range(HALF):
                        k = h * HALF + c
                        pointer = K.pointer[:, b, k, :] if k else K.pointer[:, 1 - b, G, :]
                        nc.tensor.matmul(at_ps[h][:, c, :], loT_f[:, k, :], pointer, start=True, stop=False)
                        last = nc.tensor.matmul(at_ps[h][:, c, :], same[:, k, :], hi1[:, b, k, :],
                                                start=False, stop=True)
                    last.then_inc(looked, 1)

            ahead(0, 0, True)
            look(0, 0, True)
            ahead(1, 1, False)
            look(1, 1, True)
            with pe.Fori(1, S.GROUPS // 2) as i:
                ahead(2 * i, 0, False)
                look(2 * i, 0, False)
                ahead(2 * i + 1, 1, False)
                look(2 * i + 1, 1, False)

        @block.scalar
        def _(act):
            def step(g, b, first):
                for h in range(2):
                    part = slice(h * HALF, (h + 1) * HALF)
                    act.wait_ge(turned, 2 * g + h + 1)
                    if not (first and b == 0):
                        act.wait_ge(looked, 2 * g - 1 + h)
                    nc.scalar.activation(loT_b[:, part, :], loT_ps[h][:], ACT.Copy).then_inc(loT_ok, 1)
                    nc.scalar.activation(loT_f[:, part, :], loT_ps[h][:], ACT.Copy).then_inc(loT_ok, 1)
                if not first:
                    act.wait_ge(scattered[b], (g - b) * 8 * G)
                nc.scalar.activation(dst_s[:, b, :], K.dst_i[:, bass.ds(g * G, G)], ACT.Copy).then_inc(dsts, 1)
            groups(act, step)

        @block.gpsimd
        def _(pool):
            def step(g, b, first):
                pool.wait_ge(slots, g + 1)
                pool.wait_ge(dsts, g + 1)
                pool.sem_inc(turns, 1)
                for c in range(G):
                    pool.indirect_dma_start(
                        out=K.slot_table, out_offset=bass.IndirectOffsetOnAxis(ap=slot_i[:, b, c:c + 1], axis=0),
                        in_=dst_s[:, b, c:c + 1], in_offset=None, bounds_check=S.SLOTS - 1,
                        oob_is_err=False).then_inc(scattered[b], 16)
            groups(pool, step)
            pool.wait_ge(scattered[0], 8 * G * S.GROUPS)
            pool.wait_ge(scattered[1], 8 * G * S.GROUPS)


def build_attention(nc, S, K):
    P, D, H, SL, NB, MB, T = S.P, S.D, S.H, S.SL, S.NB, S.MB, S.RT
    GATHERS = 16 * SL
    ON_DVE = SL - 1
    EARLY = 2
    with ExitStack() as ctx:
        def sb(name, shape, dt):
            return ctx.enter_context(nc.sbuf_tensor(f"att_{name}", shape, dt))

        def pb(name, shape, dt):
            return ctx.enter_context(nc.psum_tensor(f"att_{name}", shape, dt))

        def sem(name):
            return K.stack.enter_context(nc.semaphore(f"att_{name}"))

        idx = sb("idx", [P, MB, SL], I32)
        node = sb("node", [P, MB], I32)
        first_node = sb("first_node", [P, MB], I32)
        flags = sb("flags", [H, MB, P + 1], F32)
        kv = [sb(f"kv{b}", [P, SL, 2 * D], F32) for b in range(NB)]
        q = [sb(f"q{m}", [P, D], F32) for m in range(MB)]
        hotT = sb("hotT", [P, P], F32)
        prod = sb("prod", [P, SL, D], F32)
        ev = [sb(f"ev{k}", [P, SL, D], F32) for k in range(2)]
        local = sb("local", [P, NB], F32)
        onehot = sb("onehot", [P, NB, P], F32)
        absent = sb("absent", [P, SL], F32)
        raw = sb("raw", [P, SL, H], F32)
        score = sb("score", [P, NB, SL, H], F32)
        rawmax = sb("rawmax", [P, H], F32)
        rowmax = sb("rowmax", [P, NB, H], F32)
        upto = sb("upto", [H, NB, P], F32)
        top = sb("top", [H, NB, P], F32)
        drop = sb("drop", [H, NB], F32)
        shifted = sb("shifted", [P, NB, SL, H], F32)
        e = sb("e", [P, NB, SL, H], F32)
        esum = sb("esum", [P, NB, H], F32)
        fade = sb("fade", [H, NB], F32)
        fadeT = sb("fadeT", [P, NB, 2], F32)
        new_att = sb("new_att", [P, 2], F32)
        new_den = sb("new_den", [H, 1], F32)

        row_ps = pb("row_ps", [P, P + D], F32)
        hotT_ps, q_ps = row_ps[:, 0:P], row_ps[:, P:P + D]
        maxT_ps = pb("maxT_ps", [H, P], F32)
        top_ps = pb("top_ps", [P, H], F32)
        fade_ps = pb("fade_ps", [P, 2], F32)
        att_ps = [pb(f"att_ps{k}", [P, 2, P], F32) for k in range(2)]
        den_ps = [pb(f"den_ps{k}", [H, P], F32) for k in range(2)]

        tabled = [sem(f"tabled{m}") for m in range(MB)]
        gathered = [sem(f"gathered{b}") for b in range(NB)]
        windowed = [sem(f"windowed{m}") for m in range(MB)]
        padded = sem("padded")
        prep = sem("prep")
        turns, turns_pe, turns_sp = sem("turns"), sem("turns_pe"), sem("turns_sp")
        multiplied = sem("multiplied")
        reduced = sem("reduced")
        absents = sem("absents")
        scored = sem("scored")
        rawmaxed = sem("rawmaxed")
        maxed = sem("maxed")
        maxT = sem("maxT")
        scanned = sem("scanned")
        dropped = sem("dropped")
        topped = sem("topped")
        shifts = sem("shifts")
        exps = sem("exps")
        esums = sem("esums")
        weighted = sem("weighted")
        weighted_act = sem("weighted_act")
        locals_ = sem("locals")
        hot = sem("hot")
        turned = sem("turned")
        turneds = sem("turneds")
        expanded = sem("expanded")
        fades = sem("fades")
        spread = sem("spread")
        fadesT = sem("fadesT")
        summed = sem("summed")
        columns = sem("columns")
        placed = sem("placed")
        block = ctx.enter_context(nc.Block())

        def tiles(engine, step):
            for u in range(MB):
                step(0, u)
            with engine.Fori(1, T // MB) as i:
                for u in range(MB):
                    step(i, u)

        def before(i, u):
            return (i, u - 1) if u else (i - 1, MB - 1)

        def after(i, u):
            return (i, u + 1) if u < MB - 1 else (i + 1, 0)

        def turn(i, u):
            return i * (MB // NB) + u // NB

        def starts(i, u):
            return isinstance(i, int) and i == 0 and u == 0

        def has(i, u, back):
            return not isinstance(i, int) or MB * i + u >= back

        @block.sync
        def _(sp):
            sp.wait_ge(prep, NB + 6)
            sp.dma_start(K.q_dram[S.V:S.V + P, :], q[MB - 1][:]).then_inc(padded, 16)
            sp.wait_ge(padded, 16)

            def window(i, u):
                sp.wait_ge(tabled[u], 64 * (i + 1))
                sp.sem_inc(turns_sp, 1)
                n0 = sp.value_load(first_node[0:1, u:u + 1], min_val=0, max_val=S.V)
                sp.dma_start(q[u][:], K.q_dram[bass.ds(n0, P), :]).then_inc(windowed[u], 16)

            def tables(i, u, t):
                if has(i, u, MB):
                    sp.wait_ge(placed, 4 * (MB * i + u - MB + 1))
                    sp.sem_inc(turns_sp, 1)
                    sp.wait_ge(gathered[u % NB], GATHERS * (turn(i, u) - MB // NB + 1))
                    sp.sem_inc(turns_sp, 1)
                sp.dma_start(idx[:, u, :],
                             K.slot_table[bass.ds(t * (P * SL), P * SL)].rearrange("(p c) o -> p (c o)", p=P))\
                  .then_inc(tabled[u], 16)
                sp.dma_start(node[:, u:u + 1], K.node_table[bass.ds(t * P, P)].rearrange("(p o) -> p o", o=1))\
                  .then_inc(tabled[u], 16)
                sp.dma_start(first_node[:, u:u + 1],
                             K.node_table[bass.ds(t * P, 1)].rearrange("(p o) -> p o", o=1).to_broadcast([P, 1]))\
                  .then_inc(tabled[u], 16)
                sp.dma_start(flags[:, u, :],
                             K.flag_table[bass.ds(t * P, P + 1)].rearrange("(o c) -> o c", o=1).to_broadcast([H, P + 1]))\
                  .then_inc(tabled[u], 16)

            def step(i, u):
                tables(i, u, MB * i + u)
                if has(i, u, 2):
                    window(*before(*before(i, u)))
            tiles(sp, step)
            tables(T // MB, 0, T - 1)
            window(T // MB - 1, MB - 2)
            window(T // MB - 1, MB - 1)

        @block.gpsimd
        def _(pool):
            for b in range(NB):
                nc.gpsimd.memset(kv[b][:], 0.0).then_inc(prep, 1)
            nc.gpsimd.memset(upto[:, NB - 1, P - 1:P], S.EMPTY).then_inc(prep, 1)
            nc.gpsimd.memset(K.attT[:], 0.0).then_inc(prep, 1)
            nc.gpsimd.memset(K.denT[:], 0.0).then_inc(prep, 1)
            sp3 = K.spreader[:].rearrange("h (a b) -> h a b", b=S.HD)
            nc.gpsimd.memset(K.spreader[:], 0.0).then_inc(prep, 1)
            nc.gpsimd.memset(q[MB - 1][:], 0.0).then_inc(prep, 1)
            pool.wait_ge(prep, NB + 5)
            nc.gpsimd.affine_select(out=sp3, in_=sp3, compare_op=ALU.not_equal, fill=1.0, base=0,
                                    pattern=[[-1, H], [0, S.HD]], channel_multiplier=1).then_inc(prep, 1)

            def step(i, u):
                t, b = MB * i + u, u % NB
                pool.wait_ge(tabled[u], 64 * (i + 1))
                if has(i, u, NB):
                    pool.wait_ge(weighted, 2 * (t - NB + 1))
                    pool.sem_inc(turns, 1)
                    pool.wait_ge(weighted_act, t - NB + 1)
                pool.sem_inc(turns, 1)
                for j in range(SL):
                    pool.indirect_dma_start(
                        out=kv[b][:, j, :], out_offset=None, in_=K.kv_dram,
                        in_offset=bass.IndirectOffsetOnAxis(ap=idx[:, u, j:j + 1], axis=0),
                        bounds_check=S.V - 1, oob_is_err=False).then_inc(gathered[b], 16)
            tiles(pool, step)

        @block.vector
        def _(dve):
            dve.wait_ge(prep, NB + 6)

            def shift(i, u):
                t, b = MB * i + u, u % NB
                dve.wait_ge(topped, t + 1)
                if has(i, u, NB):
                    dve.wait_ge(exps, t - NB + 1)
                nc.vector.tensor_tensor(shifted[:, b], score[:, b], top_ps[:].unsqueeze(1).to_broadcast([P, SL, H]),
                                        ALU.subtract).then_inc(shifts, 1)

            def weigh(i, u, first):
                t, b = MB * i + u, u % NB
                if first and has(i, u, 2):
                    dve.wait_ge(summed, t - 1)
                slots = slice(0, EARLY) if first else slice(EARLY, ON_DVE)
                n = slots.stop - slots.start
                nc.vector.tensor_tensor(ev[u % 2][:, slots].rearrange("p s (h c) -> p s h c", h=H),
                                        kv[b][:, slots, D:2 * D].rearrange("p s (h c) -> p s h c", h=H),
                                        e[:, b, slots].unsqueeze(3).to_broadcast([P, n, H, S.HD]),
                                        ALU.mult).then_inc(weighted, 1)

            def sums(i, u):
                t, b = MB * i + u, u % NB
                dve.wait_ge(exps, t + 1)
                nc.vector.tensor_reduce(esum[:, b, :], e[:, b].rearrange("p s h -> p h s"), AX.X, ALU.add)\
                    .then_inc(esums, 1)

            def offsets(i, u):
                t, b = MB * i + u, u % NB
                dve.wait_ge(tabled[u], 64 * (i + 1))
                nc.vector.tensor_tensor(local[:, b:b + 1], node[:, u:u + 1], first_node[:, u:u + 1],
                                        ALU.subtract).then_inc(locals_, 1)

            def one_hot(i, u):
                t, b = MB * i + u, u % NB
                dve.wait_ge(locals_, t + 1)
                if has(i, u, NB):
                    dve.wait_ge(summed, t - NB + 1)
                nc.vector.tensor_scalar(onehot[:, b, :], K.iota_f[:], local[:, b:b + 1], None, ALU.is_equal)\
                    .then_inc(hot, 1)

            offsets(0, 0)
            one_hot(0, 0)

            def step(i, u):
                t, b = MB * i + u, u % NB
                pb_, pi, pu = (u - 1) % NB, *before(i, u)
                if has(i, u, 2):
                    weigh(*before(pi, pu), False)
                dve.wait_ge(gathered[b], GATHERS * (turn(i, u) + 1))
                if not starts(i, u):
                    dve.wait_ge(reduced, t)
                dve.wait_ge(expanded, t + 1)
                nc.vector.tensor_tensor(prod[:], kv[b][:, :, 0:D], q_ps.unsqueeze(1).to_broadcast([P, SL, D]),
                                        ALU.mult).then_inc(multiplied, 1)
                if not starts(i, u):
                    shift(pi, pu)
                if not starts(i, u):
                    dve.wait_ge(scored, t)
                nc.vector.tensor_scalar(absent[:], idx[:, u, :], float(S.V), S.NEG, ALU.is_ge, ALU.mult)\
                    .then_inc(absents, 1)
                offsets(*after(i, u))
                dve.wait_ge(multiplied, t + 1)
                nc.vector.tensor_reduce(raw[:].rearrange("p s h -> p (s h)"),
                                        prod[:].rearrange("p s (h c) -> p (s h) c", h=H), AX.X, ALU.add)\
                    .then_inc(reduced, 1)
                one_hot(*after(i, u))
                dve.wait_ge(reduced, t + 1)
                dve.wait_ge(absents, t + 1)
                nc.vector.tensor_tensor(score[:, b], raw[:], absent[:].unsqueeze(2).to_broadcast([P, SL, H]),
                                        ALU.add).then_inc(scored, 1)
                if not starts(i, u):
                    sums(pi, pu)
                dve.wait_ge(scored, t + 1)
                nc.vector.tensor_reduce(rawmax[:], score[:, b].rearrange("p s h -> p h s"), AX.X, ALU.max)\
                    .then_inc(rawmaxed, 1)
                dve.wait_ge(rawmaxed, t + 1)
                nc.vector.tensor_single_scalar(rowmax[:, b, :], rawmax[:], S.EMPTY, ALU.max).then_inc(maxed, 1)
                if not starts(i, u):
                    weigh(pi, pu, True)
                dve.wait_ge(maxT, t + 1)
                if not starts(i, u):
                    dve.wait_ge(scanned, 2 * t)
                nc.vector.tensor_tensor_scan(upto[:, b, :], flags[:, u, 0:P], maxT_ps[:], upto[:, pb_, P - 1:P],
                                             ALU.add, ALU.max).then_inc(scanned, 1)
                dve.wait_ge(scanned, 2 * t + 1)
                nc.vector.tensor_tensor_scan(top[:, b, ::-1], flags[:, u, P:0:-1], upto[:, b, ::-1], S.NEG,
                                             ALU.add, ALU.max).then_inc(scanned, 1)
                dve.wait_ge(scanned, 2 * t + 2)
                nc.vector.scalar_tensor_tensor(out=drop[:, b:b + 1], in0=upto[:, pb_, P - 1:P],
                                               scalar=flags[:, u, 0:1], in1=top[:, b, 0:1], op0=ALU.add,
                                               op1=ALU.subtract).then_inc(dropped, 1)
            tiles(dve, step)
            last = (T // MB - 1, MB - 1)
            weigh(*before(*last), False)
            shift(*last)
            sums(*last)
            weigh(*last, True)
            weigh(*last, False)

        @block.tensor
        def _(pe):
            pe.wait_ge(prep, NB + 6)

            def attend(i, u, k):
                t, b = MB * i + u, u % NB
                if k == 0:
                    pe.wait_ge(weighted, 2 * t + 2)
                    pe.wait_ge(weighted_act, t + 1)
                    if has(i, u, 2):
                        pe.wait_ge(placed, 4 * t - 4)
                for j in range(SL):
                    nc.tensor.matmul(att_ps[u % 2][:, k, :], ev[u % 2][:, j, k * P:(k + 1) * P], onehot[:, b, :],
                                     start=j == 0, stop=j == SL - 1)
                if k == 1:
                    nc.tensor.matmul(den_ps[u % 2][:], esum[:, b, :], onehot[:, b, :], start=True, stop=True)\
                        .then_inc(summed, 1)

            def turn_onehot(i, u):
                t, b = MB * i + u, u % NB
                pe.wait_ge(hot, t + 1)
                if not starts(i, u):
                    pe.wait_ge(multiplied, t)
                nc.tensor.transpose(hotT_ps, onehot[:, b, :], K.ident[:]).then_inc(turned, 1)

            def spread_fade(i, u):
                t, b = MB * i + u, u % NB
                pe.wait_ge(fades, t + 1)
                if not starts(i, u):
                    pe.wait_ge(fadesT, t)
                for k in range(2):
                    last = nc.tensor.matmul(fade_ps[:, k:k + 1], K.spreader[:, k * P:(k + 1) * P], fade[:, b:b + 1],
                                            start=True, stop=True)
                last.then_inc(spread, 1)

            turn_onehot(0, 0)

            def step(i, u):
                t, b = MB * i + u, u % NB
                pe.wait_ge(windowed[u], 16 * (i + 1))
                pe.wait_ge(turneds, t + 1)
                nc.tensor.matmul(q_ps, hotT[:], q[u][:], start=True, stop=True).then_inc(expanded, 1)
                if not starts(i, u):
                    spread_fade(*before(i, u))
                if has(i, u, 3):
                    attend(*before(*before(*before(i, u))), 1)
                if has(i, u, 2):
                    attend(*before(*before(i, u)), 0)
                pe.wait_ge(maxed, t + 1)
                if not starts(i, u):
                    pe.wait_ge(scanned, 2 * t)
                nc.tensor.transpose(maxT_ps[:], rowmax[:, b, :], K.ident[:]).then_inc(maxT, 1)
                turn_onehot(*after(i, u))
                pe.wait_ge(scanned, 2 * t + 2)
                if not starts(i, u):
                    pe.wait_ge(shifts, t)
                pe.sem_inc(turns_pe, 1)
                nc.tensor.transpose(top_ps[:], top[:, b, :], K.ident[0:H, 0:H]).then_inc(topped, 1)
            tiles(pe, step)
            spread_fade(T // MB - 1, MB - 1)
            attend(T // MB - 1, MB - 3, 1)
            for u in (MB - 2, MB - 1):
                for k in range(2):
                    attend(T // MB - 1, u, k)

        @block.scalar
        def _(act):
            act.wait_ge(prep, NB + 6)

            def exponentials(i, u):
                t, b = MB * i + u, u % NB
                act.wait_ge(shifts, t + 1)
                if has(i, u, NB):
                    act.wait_ge(weighted, 2 * (t - NB + 1))
                nc.scalar.activation(e[:, b], shifted[:, b], ACT.Exp).then_inc(exps, 1)
                act.wait_ge(exps, t + 1)
                if has(i, u, 2):
                    act.wait_ge(summed, t - 1)
                for j in range(ON_DVE, SL):
                    for h in range(H):
                        last = nc.scalar.activation(ev[u % 2][:, j, h * S.HD:(h + 1) * S.HD],
                                                    kv[b][:, j, D + h * S.HD:D + (h + 1) * S.HD], ACT.Copy,
                                                    scale=e[:, b, j, h:h + 1])
                last.then_inc(weighted_act, 1)

            def copy_onehot(t):
                act.wait_ge(turned, t + 1)
                act.wait_ge(expanded, t)
                nc.scalar.activation(hotT[:], hotT_ps, ACT.Copy).then_inc(turneds, 1)

            def place(i, u):
                t, b = MB * i + u, u % NB
                n0 = act.value_load(first_node[0:1, u:u + 1], min_val=0, max_val=S.V)
                act.wait_ge(summed, t + 1)
                nc.scalar.activation(new_att[:], att_ps[u % 2][:, :, 0], ACT.Copy).then_inc(columns, 1)
                nc.scalar.activation(new_den[:], den_ps[u % 2][:, 0:1], ACT.Copy).then_inc(columns, 1)
                nc.scalar.activation(K.attT[:, :, bass.ds(n0 + 1, P - 1)], att_ps[u % 2][:, :, 1:P], ACT.Copy)
                nc.scalar.activation(K.denT[:, bass.ds(n0 + 1, P - 1)], den_ps[u % 2][:, 1:P], ACT.Copy).then_inc(placed, 1)
                act.wait_ge(columns, 2 * t + 2)
                for k in range(2):
                    nc.scalar.activation(K.attT[:, k, bass.ds(n0, 1)], K.attT[:, k, bass.ds(n0, 1)], ACT.Identity,
                                         bias=new_att[:, k:k + 1], scale=fadeT[:, b, k:k + 1]).then_inc(placed, 1)
                nc.scalar.activation(K.denT[:, bass.ds(n0, 1)], K.denT[:, bass.ds(n0, 1)], ACT.Identity,
                                     bias=new_den[:], scale=fade[:, b:b + 1]).then_inc(placed, 1)
                act.wait_ge(placed, 4 * t + 4)

            def copy_fade(i, u):
                t, b = MB * i + u, u % NB
                act.wait_ge(spread, t + 1)
                nc.scalar.activation(fadeT[:, b, :], fade_ps[:], ACT.Copy).then_inc(fadesT, 1)

            act.wait_ge(turned, 1)
            nc.scalar.activation(hotT[:], hotT_ps, ACT.Copy).then_inc(turneds, 1)

            def step(i, u):
                t, b = MB * i + u, u % NB
                if not starts(i, u):
                    copy_fade(*before(i, u))
                    exponentials(*before(i, u))
                if has(i, u, 3):
                    place(*before(*before(*before(i, u))))
                copy_onehot(t + 1)
                act.wait_ge(dropped, t + 1)
                nc.scalar.activation(fade[:, b:b + 1], drop[:, b:b + 1], ACT.Exp).then_inc(fades, 1)
            tiles(act, step)
            copy_fade(T // MB - 1, MB - 1)
            exponentials(T // MB - 1, MB - 1)
            place(T // MB - 1, MB - 3)
            place(T // MB - 1, MB - 2)
            place(T // MB - 1, MB - 1)


def build_dense(nc, S, K, A, out):
    P, D, H = S.P, S.D, S.H
    TN, NT = S.TN, S.NT
    N = TN * NT
    GR = S.V // N
    FF = A.w_i.shape[1]
    FC = FF // P
    NE, E1, E2 = A.e_w1.shape[0], A.e_w1.shape[2], A.e_w2.shape[2]
    M1, M2 = A.s_w1.shape[1], A.s_w2.shape[1]
    assert GR * N == S.V and GR % 2 == 1 and E1 == P and M2 == P and M1 == 2 * P and D == 2 * P
    with ExitStack() as ctx:
        def sb(name, shape, dt):
            return ctx.enter_context(nc.sbuf_tensor(f"mlp_{name}", shape, dt))

        def pb(name, shape, dt):
            return ctx.enter_context(nc.psum_tensor(f"mlp_{name}", shape, dt))

        def sem(name):
            return K.stack.enter_context(nc.semaphore(f"mlp_{name}"))

        w_o = sb("w_o", [P, 2, D], F32)
        w_i = sb("w_i", [P, 2, FF], F32)
        w_2 = sb("w_2", [P, FC, D], F32)
        s_w1 = sb("s_w1", [P, 2, M1], F32)
        s_w2 = sb("s_w2", [P, 2, M2], F32)
        s_w3 = sb("s_w3", [P, D], F32)
        e_w1 = sb("e_w1", [P, NE, 2, E1], F32)
        e_w2 = sb("e_w2", [P, NE, E2], F32)
        e_w3 = sb("e_w3", [E2 + 1, NE, D], F32)
        g_w = sb("g_w", [P, 2, NE], F32)
        s_b1 = sb("s_b1", [P, 2], F32)
        s_b2 = sb("s_b2", [P, 1], F32)
        s_b3 = sb("s_b3", [1, D], F32)
        e_b1 = sb("e_b1", [P, NE], F32)
        e_b2 = sb("e_b2", [E2, NE], F32)
        g_b = sb("g_b", [P, NE], F32)
        gains = sb("gains", [P, 4, D], F32)
        ones = sb("ones", [1, P], F32)
        minus_half = sb("minus_half", [P, NT], F32)
        earlier = sb("earlier", [P, NE, NE], F32)

        h = sb("h", [TN, 2, NT, D], F32)
        xr = sb("xr", [TN, 2, NT, D], F32)
        attn = sb("attn", [P, 2, N], F32)
        z = sb("z", [TN, NT, D], F32)
        stats = sb("stats", [TN, NT, 6], F32)
        mv = sb("mv", [TN, NT, 2], F32)
        var = sb("var", [TN, NT], F32)
        rstd = sb("rstd", [TN, NT], F32)
        pre = sb("pre", [TN, 2, NT, D], F32)
        preT = sb("preT", [P, 2, N], F32)
        inter = sb("inter", [P, FC, N], F32)
        z2 = sb("z2", [TN, NT, D], F32)
        x1 = sb("x1", [TN, 2, NT, D], F32)
        xn = sb("xn", [TN, 2, NT, D], F32)
        xnT = sb("xnT", [P, 2, N], F32)
        h1 = sb("h1", [P, 2, N], F32)
        h2 = sb("h2", [P, N], F32)
        a1 = sb("a1", [P, NE, N], F32)
        a2 = sb("a2", [E2 + 1, NE, N], F32)
        lg = sb("lg", [TN, NT, NE], F32)
        g1 = sb("g1", [TN, NT], F32)
        g2 = sb("g2", [TN, NT, NE], F32)
        g3 = sb("g3", [TN, NT, NE], F32)
        pg = sb("pg", [TN, NT, NE], F32)
        beats = sb("beats", [TN, NT, NE, NE], F32)
        ties = sb("ties", [TN, NT, NE, NE], F32)
        wt = sb("wt", [TN, NT, NE], F32)
        res = sb("res", [TN, 2, NT, D], F32)

        den_ps = pb("den_ps", [P, 2, N], F32)
        ya_ps = pb("ya_ps", [TN, NT, D], F32)
        yb_ps = pb("yb_ps", [TN, NT, D], F32)
        tr_ps = pb("tr_ps", [P, 2, N], F32)
        mm_ps = [pb(f"mm_ps{i}", [P, 2, D], F32) for i in range(2)]
        o_ps = [pb(f"o_ps{i}", [TN, 2, D], F32) for i in range(2)]

        weights, bias_in, consts, rden = sem("weights"), sem("bias_in"), sem("consts"), sem("rden")
        in_h = [sem("in_h0"), sem("in_h1")]
        in_x = [sem("in_x0"), sem("in_x1")]
        out_done = [sem("out_done0"), sem("out_done1")]
        turns, turns_pe, turns_pool = sem("turns"), sem("turns_pe"), sem("turns_pool")
        spread = sem("spread")
        normed = sem("normed")
        projected = sem("projected")
        zs = sem("zs")
        step_v = sem("step_v")
        vars_ = sem("vars")
        rstds = sem("rstds")
        pres = sem("pres")
        preTs = sem("preTs")
        copied = sem("copied")
        mms = sem("mms")
        acts = sem("acts")
        downs = sem("downs")
        x1s = sem("x1s")
        xns = sem("xns")
        logits = sem("logits")
        lgs = sem("lgs")
        ex_in, ex_out = sem("ex_in"), sem("ex_out")
        outs = sem("outs")
        results = sem("results")
        block = ctx.enter_context(nc.Block())

        FM = FC // 2
        EM = 1 + 1 + 2 + 2
        MM = FM + EM

        def groups(engine, step):
            step(0, 0, True, False)
            step(1, 1, True, True)
            step(2, 0, True, True)
            with engine.Fori(1, (GR - 3) // 2) as i:
                step(2 * i + 1, 1, True, True)
                step(2 * i + 2, 0, True, True)
            step(GR - 2, 1, True, True)
            step(GR - 1, 0, False, True)
            step(GR, 1, False, True)

        def is_int(g, n):
            return isinstance(g, int) and g == n

        def mm_base(g, second):
            if second:
                return (g + 2) * FM + g * EM if not is_int(g, GR - 1) else GR * FM + (GR - 1) * EM
            return g * FM + (g - 1) * EM if not is_int(g, 0) else 0

        def out_banks(j):
            one, two = (o_ps, mm_ps)[j]
            return one[0:TN], two[0:TN], ya_ps[:, j, :]

        @block.sync
        def _(sp):
            def load(dst, src_):
                sp.dma_start(dst, src_).then_inc(weights, 16)

            load(w_o[:], A.w_o.rearrange("(k p) n -> p k n", p=P))
            load(w_i[:], A.w_i.rearrange("(k p) n -> p k n", p=P))
            load(w_2[:], A.w_out2.rearrange("(k p) n -> p k n", p=P))
            load(s_w1[:], A.s_w1.rearrange("(k p) n -> p k n", p=P))
            load(s_w2[:], A.s_w2.rearrange("(k p) n -> p k n", p=P))
            load(s_w3[:], A.s_w3)
            for e in range(NE):
                load(e_w1[:, e], A.e_w1[e].rearrange("(k p) n -> p k n", p=P))
                load(e_w2[:, e], A.e_w2[e])
                load(e_w3[0:E2, e], A.e_w3[e])
                load(e_b1[:, e:e + 1], A.e_b1[e].rearrange("(p o) -> p o", o=1))
                load(e_b2[:, e:e + 1], A.e_b2[e].rearrange("(p o) -> p o", o=1))
            load(e_w3[E2:E2 + 1], A.e_b3.rearrange("(o e) n -> o e n", o=1))
            load(g_w[:], A.g_w.rearrange("(k p) n -> p k n", p=P))
            for k in range(2):
                load(s_b1[:, k:k + 1], A.s_b1[k * P:(k + 1) * P].rearrange("(p o) -> p o", o=1))
            load(s_b2[:], A.s_b2.rearrange("(p o) -> p o", o=1))
            load(s_b3[:], A.s_b3.rearrange("(o n) -> o n", o=1))
            load(g_b[:], A.g_b.rearrange("(o n) -> o n", o=1).to_broadcast([P, NE]))
            for i, v in enumerate((A.ln1_g, A.ln1_b, A.ln2_g, A.ln2_b)):
                load(gains[:, i, :], v.rearrange("(o n) -> o n", o=1).to_broadcast([P, D]))

            def fetch(g, b, again):
                rows = bass.ds(g * N, N)
                if again:
                    sp.wait_ge(zs, g - 1)
                    sp.wait_ge(x1s, g - 1)
                    sp.sem_inc(turns_pool, 1)
                sp.dma_start(h[:, b], K.h_dram[rows, :].rearrange("(j p) n -> p j n", p=TN)).then_inc(in_h[b], 16)
                sp.dma_start(xr[:, b], A.x[rows, :].rearrange("(j p) n -> p j n", p=TN)).then_inc(in_x[b], 16)

            def store(g, b):
                sp.wait_ge(results, NT * g + NT)
                sp.sem_inc(turns_pool, 1)
                sp.dma_start(out[bass.ds(g * N, N), :].rearrange("(j p) n -> p j n", p=TN), res[:, b])\
                  .then_inc(out_done[b], 16)

            fetch(0, 0, False)
            fetch(1, 1, False)

            def step(g, b, more, back):
                if more and not is_int(g, GR - 2):
                    fetch(g + 2, b, True)
                if back:
                    store(g - 1, 1 - b)
            groups(sp, step)
            sp.wait_ge(out_done[0], 16 * ((GR + 1) // 2))
            sp.wait_ge(out_done[1], 16 * (GR // 2))

        WEIGHTS = 16 * (6 + 5 * NE + 7 + 4)

        @block.gpsimd
        def _(pool):
            nc.gpsimd.memset(ones[:], 1.0).then_inc(consts, 1)
            nc.gpsimd.memset(minus_half[:], -0.5).then_inc(consts, 1)
            nc.gpsimd.memset(earlier[:], 1.0).then_inc(consts, 1)
            pool.wait_ge(consts, 3)
            nc.gpsimd.memset(a2[E2:E2 + 1], 1.0).then_inc(consts, 1)
            pool.wait_ge(consts, 4)
            nc.gpsimd.affine_select(out=earlier[:], in_=earlier[:], compare_op=ALU.is_gt, fill=0.0, base=0,
                                    pattern=[[1, NE], [-1, NE]], channel_multiplier=0).then_inc(consts, 1)

            def power(n):
                pool.wait_ge(vars_, n)
                pool.sem_inc(turns_pool, 1)
                nc.gpsimd.tensor_tensor(rstd[:], var[:], minus_half[0:TN, :], ALU.pow).then_inc(rstds, 1)

            power(1)

            def step(g, b, more, back):
                if not is_int(g, GR):
                    power(3 * g + 2)
                    power(3 * g + 3)
                if more:
                    power(3 * g + 4)
            groups(pool, step)

        @block.vector
        def _(dve):
            dve.wait_ge(consts, 5)
            nc.vector.tensor_single_scalar(K.denT[:], K.denT[:], 0.5, ALU.max).then_inc(rden, 1)
            dve.wait_ge(rden, 1)
            nc.vector.reciprocal(K.denT[:], K.denT[:]).then_inc(rden, 1)
            dve.wait_ge(weights, WEIGHTS)

            class Chain:
                def __init__(self, start):
                    self.at = start

                def then(self, ins):
                    self.at = self.at + 1
                    ins.then_inc(step_v, 1)
                    dve.wait_ge(step_v, self.at)

            def normalise(c, v, o, count, eps, gain):
                for j in range(NT):
                    last = nc.vector.bn_stats(stats[:, j, :], v[:, j, :])
                c.then(last)
                dve.sem_inc(turns, 1)
                for j in range(NT):
                    last = nc.vector.bn_aggr(mv[:, j, :], stats[:, j, :])
                c.then(last)
                nc.vector.tensor_single_scalar(var[:], mv[:, :, 1], eps, ALU.add).then_inc(vars_, 1)
                dve.wait_ge(rstds, count)
                for j in range(NT):
                    last = nc.vector.tensor_scalar(o[:, j, :], v[:, j, :], mv[:, j, 0:1], rstd[:, j:j + 1],
                                                   ALU.subtract, ALU.mult)
                if gain is None:
                    return last
                c.then(last)
                gb = [gains[0:TN, gain + i, :].unsqueeze(1).to_broadcast([TN, NT, D]) for i in range(2)]
                c.then(nc.vector.tensor_tensor(o, o, gb[0], ALU.mult))
                return nc.vector.tensor_tensor(o, o, gb[1], ALU.add)

            def spread_out(g):
                dve.wait_ge(spread, g + 1)
                if not is_int(g, 0):
                    dve.wait_ge(projected, g)
                nc.vector.tensor_tensor(attn[:], K.attT[:, :, bass.ds(g * N, N)], den_ps[:], ALU.mult)\
                    .then_inc(normed, 1)

            def first_norm(g, b, c):
                dve.wait_ge(projected, g + 1)
                dve.wait_ge(in_h[b], (g - b) * 8 + 16)
                nc.vector.tensor_tensor(z[:], ya_ps[:], h[:, b], ALU.add).then_inc(zs, 1)
                dve.wait_ge(zs, g + 1)
                normalise(c, z[:], pre[:, b], 3 * g + 1, 1e-12, 0).then_inc(pres, 1)

            def second_norm(g, b, c):
                dve.wait_ge(downs, g + 1)
                dve.wait_ge(pres, g + 1)
                c.then(nc.vector.tensor_tensor(z2[:], yb_ps[:], pre[:, b], ALU.add))
                dve.wait_ge(in_x[b], (g - b) * 8 + 16)
                c.then(normalise(c, z2[:], z2[:], 3 * g + 2, 1e-12, 2))
                nc.vector.tensor_tensor(x1[:, b], z2[:], xr[:, b], ALU.add).then_inc(x1s, 1)
                dve.wait_ge(x1s, g + 1)
                if not (is_int(g, 0) or is_int(g, 1)):
                    dve.wait_ge(preTs, 2 * g - 2)
                normalise(c, x1[:, b], xn[:, b], 3 * g + 3, 1e-5, None).then_inc(xns, 1)

            wide = g1[:].unsqueeze(2).to_broadcast([TN, NT, NE])

            def gates(g, c):
                dve.wait_ge(logits, g + 1)
                c.then(nc.vector.tensor_tensor(lg[:], yb_ps[:, :, 0:NE],
                                               g_b[0:TN, :].unsqueeze(1).to_broadcast([TN, NT, NE]), ALU.add))
                c.then(nc.vector.tensor_reduce(g1[:], lg[:], AX.X, ALU.max))
                nc.vector.tensor_tensor(g2[:], lg[:], wide, ALU.subtract).then_inc(ex_in, 1)
                dve.wait_ge(ex_out, 2 * g + 1)
                c.then(nc.vector.tensor_reduce(g1[:], g3[:], AX.X, ALU.add))
                c.then(nc.vector.reciprocal(g1[:], g1[:]))
                c.then(nc.vector.tensor_tensor(pg[:], g3[:], wide, ALU.mult))
                c.then(nc.vector.tensor_reduce(g1[:], pg[:], AX.X, ALU.max))
                nc.vector.tensor_tensor(g2[:], pg[:], wide, ALU.subtract).then_inc(ex_in, 1)
                mine = pg[:].unsqueeze(3).to_broadcast([TN, NT, NE, NE])
                other = pg[:].unsqueeze(2).to_broadcast([TN, NT, NE, NE])
                c.then(nc.vector.tensor_tensor(beats[:], other, mine, ALU.is_gt))
                c.then(nc.vector.tensor_tensor(ties[:], other, mine, ALU.is_equal))
                c.then(nc.vector.tensor_tensor(ties[:], ties[:],
                                               earlier[0:TN].unsqueeze(1).to_broadcast([TN, NT, NE, NE]), ALU.mult))
                c.then(nc.vector.tensor_tensor(beats[:], beats[:], ties[:], ALU.add))
                c.then(nc.vector.tensor_reduce(wt[:], beats[:], AX.X, ALU.add))
                c.then(nc.vector.tensor_single_scalar(wt[:], wt[:], 2.0, ALU.is_lt))

            def gate_weights(g, c):
                dve.wait_ge(ex_out, 2 * g + 2)
                c.then(nc.vector.tensor_tensor(wt[:], wt[:], g3[:], ALU.mult))
                c.then(nc.vector.tensor_reduce(g1[:], wt[:], AX.X, ALU.add))
                c.then(nc.vector.reciprocal(g1[:], g1[:]))
                nc.vector.tensor_tensor(wt[:], wt[:], wide, ALU.mult).then_inc(lgs, 1)

            def finish(g, b, c):
                dve.wait_ge(lgs, g + 1)
                if not (is_int(g, 0) or is_int(g, 1)):
                    dve.wait_ge(out_done[b], (g - b) * 8)
                for j in range(NT):
                    r = res[:, b, j, :]
                    one, two, three = out_banks(j)
                    dve.wait_ge(outs, 2 * NT * g + 2 * j + 1)
                    c.then(nc.vector.tensor_tensor(r, one[:, 0, :], x1[:, b, j, :], ALU.add))
                    for o, e in ((one[:, 1, :], 0), (two[:, 0, :], 1), (two[:, 1, :], 2), (three, 3)):
                        if e == 1:
                            dve.wait_ge(outs, 2 * NT * g + 2 * j + 2)
                        last = nc.vector.scalar_tensor_tensor(out=r, in0=o, scalar=wt[:, j, e:e + 1], in1=r,
                                                              op0=ALU.mult, op1=ALU.add)
                        if e < NE - 1:
                            c.then(last)
                    last.then_inc(results, 1)

            LA = 4
            LB = 1 + 5 + 2
            LC = 15 + NE * NT

            spread_out(0)
            first_norm(0, 0, Chain(0))

            def step(g, b, more, back):
                base = LA + g * (LA + LB) + (0 if is_int(g, 0) else (g - 1) * LC)
                if is_int(g, GR):
                    base = LA * GR + LB * GR + (GR - 1) * LC
                if more:
                    spread_out(g + 1)
                c = Chain(base)
                if back:
                    gates(g - 1, c)
                if not is_int(g, GR):
                    second_norm(g, b, c)
                if more:
                    first_norm(g + 1, 1 - b, c)
                if back:
                    gate_weights(g - 1, c)
                    finish(g - 1, 1 - b, c)
                want = base + (0 if is_int(g, GR) else LB) + (LA if more else 0) + (LC if back else 0)
                if isinstance(g, int):
                    assert c.at == want, (g, c.at, want)
            groups(dve, step)

        @block.tensor
        def _(pe):
            pe.wait_ge(weights, WEIGHTS)
            pe.wait_ge(consts, 5)
            pe.wait_ge(rden, 2)

            def spread_sums(g):
                if not is_int(g, 0):
                    pe.wait_ge(normed, g)
                for k in range(2):
                    last = nc.tensor.matmul(den_ps[:, k, :], K.spreader[:, k * P:(k + 1) * P],
                                            K.denT[:, bass.ds(g * N, N)], start=True, stop=True)
                last.then_inc(spread, 1)

            def project(g):
                pe.wait_ge(normed, g + 1)
                if not is_int(g, 0):
                    pe.wait_ge(zs, g)
                if not (is_int(g, 0) or is_int(g, 1) or is_int(g, 2)):
                    pe.wait_ge(results, NT * g - 2 * NT)
                for j in range(NT):
                    for k in range(2):
                        last = nc.tensor.matmul(ya_ps[:, j, :], attn[:, k, j * TN:(j + 1) * TN], w_o[:, k, :],
                                                start=k == 0, stop=k == 1)
                last.then_inc(projected, 1)

            def turn(rows, count):
                pe.sem_inc(turns_pe, 1)
                for j in range(NT):
                    for k in range(2):
                        last = nc.tensor.transpose(tr_ps[:, k, j * TN:(j + 1) * TN], rows[:, j, k * P:(k + 1) * P],
                                                   K.ident[0:TN, 0:TN])
                last.then_inc(preTs, 1)
                pe.wait_ge(copied, count)

            def mm_free(n, none=False):
                if not none:
                    pe.wait_ge(acts, n - 1)

            def gelu_layer(g, b):
                pe.wait_ge(pres, g + 1)
                turn(pre[:, b], 2 * g + 1)
                at = mm_base(g, False)
                if not (is_int(g, 0) or is_int(g, 1)):
                    pe.wait_ge(results, NT * g - NT)
                for m in range(FM):
                    mm_free(at + m, is_int(g, 0) and m < 2)
                    for i in range(2):
                        for k in range(2):
                            c = 2 * m + i
                            last = nc.tensor.matmul(mm_ps[m % 2][:, i, 0:N], w_i[:, k, c * P:(c + 1) * P],
                                                    preT[:, k, :], start=k == 0, stop=k == 1)
                    last.then_inc(mms, 1)
                if not is_int(g, 0):
                    pe.wait_ge(x1s, g)
                    pe.wait_ge(ex_in, 2 * g - 1)
                pe.wait_ge(acts, at + FM)
                for j in range(NT):
                    for c in range(FC):
                        last = nc.tensor.matmul(yb_ps[:, j, :], inter[:, c, j * TN:(j + 1) * TN], w_2[:, c, :],
                                                start=c == 0, stop=c == FC - 1)
                last.then_inc(downs, 1)

            def gate_logits(g, b):
                pe.wait_ge(xns, g + 1)
                turn(xn[:, b], 2 * g + 2)
                pe.wait_ge(x1s, g + 1)
                for j in range(NT):
                    for k in range(2):
                        last = nc.tensor.matmul(yb_ps[:, j, 0:NE], xnT[:, k, j * TN:(j + 1) * TN], g_w[:, k, :],
                                                start=k == 0, stop=k == 1)
                last.then_inc(logits, 1)

            def experts(g, b, more):
                at = mm_base(g, True)

                def pair(m, parts):
                    mm_free(at + m)
                    for i, p in enumerate(parts):
                        for k, (w, v) in enumerate(p):
                            last = nc.tensor.matmul(mm_ps[m % 2][0:w.shape[-1], i, 0:N], w, v,
                                                    start=k == 0, stop=k == len(p) - 1)
                    last.then_inc(mms, 1)

                both = (0, 1)
                if is_int(g, GR - 1):
                    pe.wait_ge(results, NT * g)
                pair(0, [[(s_w1[:, k, i * P:(i + 1) * P], xnT[:, k, :]) for k in both] for i in both])
                pair(1, [[(e_w1[:, e, k, :], xnT[:, k, :]) for k in both] for e in (0, 1)])
                pair(2, [[(e_w1[:, e, k, :], xnT[:, k, :]) for k in both] for e in (2, 3)])
                pair(3, [[(s_w2[:, k, :], h1[:, k, :]) for k in both]])
                pe.wait_ge(acts, at + 2)
                pair(4, [[(e_w2[:, e, :], a1[:, e, :])] for e in (0, 1)])
                pe.wait_ge(acts, at + 3)
                pair(5, [[(e_w2[:, e, :], a1[:, e, :])] for e in (2, 3)])
                pe.wait_ge(acts, at + 6)
                if not is_int(g, 0):
                    pe.wait_ge(results, NT * g)
                if more:
                    pe.wait_ge(zs, g + 3)
                elif is_int(g, GR - 2):
                    pe.wait_ge(zs, GR)
                for j in range(NT):
                    nc.tensor.matmul(ya_ps[:, j, :], a2[:, NE - 1, j * TN:(j + 1) * TN], e_w3[:, NE - 1, :],
                                     start=True, stop=True)
                for j in range(NT):
                    nodes = slice(j * TN, (j + 1) * TN)
                    one, two, _ = out_banks(j)
                    nc.tensor.matmul(one[:, 0, :], h2[:, nodes], s_w3[:], start=True, stop=False)
                    nc.tensor.matmul(one[:, 0, :], ones[:, 0:TN], s_b3[:], start=False, stop=True)
                    for o, e in ((one[:, 1, :], 0), (two[:, 0, :], 1), (two[:, 1, :], 2)):
                        last = nc.tensor.matmul(o, a2[:, e, nodes], e_w3[:, e, :], start=True, stop=True)
                        if e != 1:
                            last.then_inc(outs, 1)

            spread_sums(0)
            project(0)

            def step(g, b, more, back):
                if more:
                    spread_sums(g + 1)
                if back:
                    gate_logits(g - 1, 1 - b)
                if not is_int(g, GR):
                    gelu_layer(g, b)
                if more:
                    project(g + 1)
                if back:
                    experts(g - 1, 1 - b, more)
            groups(pe, step)

        @block.scalar
        def _(act):
            act.wait_ge(weights, WEIGHTS)
            act.wait_ge(consts, 5)

            def step(g, b, more, back):
                p = g - 1
                if back:
                    act.wait_ge(preTs, 2 * p + 2)
                    nc.scalar.activation(xnT[:], tr_ps[:], ACT.Copy).then_inc(copied, 1)
                if not is_int(g, GR):
                    act.wait_ge(preTs, 2 * g + 1)
                    nc.scalar.activation(preT[:], tr_ps[:], ACT.Copy).then_inc(copied, 1)
                if back:
                    act.wait_ge(ex_in, 2 * p + 1)
                    nc.scalar.activation(g3[:], g2[:], ACT.Exp).then_inc(ex_out, 1)
                if not is_int(g, GR):
                    at = mm_base(g, False)
                    for m in range(FM):
                        act.wait_ge(mms, at + m + 1)
                        if m == 0 and not is_int(g, 0):
                            act.wait_ge(downs, g)
                        nc.scalar.activation(inter[:, 2 * m:2 * m + 2, :], mm_ps[m % 2][:, :, 0:N], ACT.Gelu)\
                            .then_inc(acts, 1)
                if back:
                    at = mm_base(p, True)
                    act.wait_ge(ex_in, 2 * p + 2)
                    nc.scalar.activation(g3[:], g2[:], ACT.Exp).then_inc(ex_out, 1)
                    act.wait_ge(mms, at + 1)
                    for i in range(2):
                        last = nc.scalar.activation(h1[:, i, :], mm_ps[0][:, i, 0:N], ACT.Relu, bias=s_b1[:, i:i + 1])
                    last.then_inc(acts, 1)
                    for m in (1, 2):
                        act.wait_ge(mms, at + m + 1)
                        for i in range(2):
                            e = 2 * (m - 1) + i
                            last = nc.scalar.activation(a1[:, e, :], mm_ps[m % 2][:, i, 0:N], ACT.Relu,
                                                        bias=e_b1[:, e:e + 1])
                        last.then_inc(acts, 1)
                    act.wait_ge(mms, at + 4)
                    nc.scalar.activation(h2[:], mm_ps[1][:, 0, 0:N], ACT.Relu, bias=s_b2[:]).then_inc(acts, 1)
                    for m in (4, 5):
                        act.wait_ge(mms, at + m + 1)
                        for i in range(2):
                            e = 2 * (m - 4) + i
                            last = nc.scalar.activation(a2[0:E2, e, :], mm_ps[m % 2][0:E2, i, 0:N], ACT.Relu,
                                                        bias=e_b2[:, e:e + 1])
                        last.then_inc(acts, 1)
            groups(act, step)


class Kept:
    pass


def bass_gnn_ffn(nc, x, src, dst, w_qkv, w_o, ln1_g, ln1_b, w_i, w_out2, ln2_g, ln2_b, s_w1, s_b1, s_w2, s_b2,
                 s_w3, s_b3, e_w1, e_b1, e_w2, e_b2, e_w3, e_b3, g_w, g_b, out):
    S = Shape(x.shape[0], src.shape[0], x.shape[1], 8)
    K = Kept()
    A = Kept()
    A.x, A.w_o, A.ln1_g, A.ln1_b, A.w_i, A.w_out2, A.ln2_g, A.ln2_b = x, w_o, ln1_g, ln1_b, w_i, w_out2, ln2_g, ln2_b
    A.s_w1, A.s_b1, A.s_w2, A.s_b2, A.s_w3, A.s_b3 = s_w1, s_b1, s_w2, s_b2, s_w3, s_b3
    A.e_w1, A.e_b1, A.e_w2, A.e_b2, A.e_w3, A.e_b3, A.g_w, A.g_b = e_w1, e_b1, e_w2, e_b2, e_w3, e_b3, g_w, g_b
    K.h_dram = nc.dram_tensor("h_rows", [S.V, S.D], F32).ap()
    K.q_dram = nc.dram_tensor("q_rows", [S.V + S.P, S.D], F32).ap()
    K.kv_dram = nc.dram_tensor("kv_rows", [S.V, 2 * S.D], F32).ap()
    K.slot_table = nc.dram_tensor("slot_table", [S.SLOTS, 1], I32).ap()
    K.mark_table = nc.dram_tensor("mark_table", [S.ROWS, 1], F32).ap()
    K.flag_table = nc.dram_tensor("flag_table", [S.ROWS + 1], F32).ap()
    K.node_table = nc.dram_tensor("node_table", [S.ROWS], I32).ap()
    with ExitStack() as ctx:
        K.stack = ctx
        def sb(name, shape, dt, into=ctx):
            return into.enter_context(nc.sbuf_tensor(name, shape, dt))

        K.ident = sb("ident", [S.P, S.P], F32)
        K.ident_b = sb("ident_b", [S.P, S.P], BF16)
        K.before = sb("before", [S.P, S.P], F32)
        K.before_b = sb("before_b", [S.P, S.P], BF16)
        K.iota_i = sb("iota_i", [S.P, S.P], I32)
        K.iota_b = sb("iota_b", [S.P, S.P], BF16)
        K.iota_f = sb("iota_f", [S.P, S.P], F32)
        K.is_node = sb("is_node", [S.P, S.BLK], F32)
        with ExitStack() as edges:
            K.dst_i = sb("dst_i", [S.P, S.EC], I32, edges)
            K.hi = sb("hi", [S.P, S.EC + S.G], BF16, edges)
            K.lo = sb("lo", [S.P, S.EC + S.G], BF16, edges)
            K.pad = sb("pad", [S.P, S.EC], BF16, edges)
            K.degree = sb("degree", [S.P, S.BLK], F32, edges)
            K.pointer = sb("pointer", [S.P, 2, S.G + 1, S.BLK], F32, edges)
            build_prepare(nc, S, K, x, src, dst, w_qkv)
            build_rows(nc, S, K)
            build_slots(nc, S, K)
        K.attT = sb("attT", [S.P, 2, S.V + S.P], F32)
        K.denT = sb("denT", [S.H, S.V + S.P], F32)
        K.spreader = sb("spreader", [S.H, S.D], F32)
        build_attention(nc, S, K)
        build_dense(nc, S, K, A, out)


_INS = ["x", "src", "dst", "L0_gnn_W_qkv", "L0_gnn_W_o", "L0_gnn_ln1_g", "L0_gnn_ln1_b", "L0_gnn_W_i",
        "L0_gnn_W_out2", "L0_gnn_ln2_g", "L0_gnn_ln2_b", "L0_ffn_sW1", "L0_ffn_sb1", "L0_ffn_sW2", "L0_ffn_sb2",
        "L0_ffn_sW3", "L0_ffn_sb3", "L0_ffn_eW1", "L0_ffn_eb1", "L0_ffn_eW2", "L0_ffn_eb2", "L0_ffn_eW3",
        "L0_ffn_eb3", "L0_ffn_gW", "L0_ffn_gb"]


def kernel(**inputs):
    import numpy as _np
    import concourse.bacc as _bacc
    from concourse import mybir as _mybir
    from concourse.bass_utils import run_bass_kernel_spmd as _run

    nc = _bacc.Bacc("TRN2", target_bir_lowering=False, num_devices=1)
    arrays, args = {}, []
    for name in _INS:
        a = _np.ascontiguousarray(inputs[name])
        arrays[f"in_{name}_dram"] = a
        args.append(nc.dram_tensor(f"in_{name}_dram", a.shape, _mybir.dt.from_np(a.dtype), kind="ExternalInput").ap())
    x = inputs["x"]
    out = nc.dram_tensor("out_0_dram", x.shape, _mybir.dt.from_np(_np.dtype("float32")), kind="ExternalOutput").ap()
    bass_gnn_ffn(nc, *args, out)
    r = _run(nc, [arrays], core_ids=[0])
    return r.results[0]["out_0_dram"]
```
